# Optimizing a Trainium2 kernel written in Bass

```python
import numpy as np
import jax
import jax.numpy as jnp

def _softmax(x, axis=-1):
    return jax.nn.softmax(x, axis=axis)

def _gelu(x):
    return jax.nn.gelu(x, approximate=True)

def _silu(x):
    return jax.nn.silu(x)

def _sigmoid(x):
    return jax.nn.sigmoid(x)

def _layernorm(x, axis=-1, eps=1e-05):
    m = jnp.mean(x, axis=axis, keepdims=True)
    v = jnp.var(x, axis=axis, keepdims=True)
    return (x - m) / jnp.sqrt(v + eps)

def _scatter_add(tgt, idx, src, axis=0):
    return tgt.at[idx].add(src)

def _segment_sum(src, seg, n):
    return jax.ops.segment_sum(src, seg, n)
kernel_name = 'mk_decoder_preln_d1_seqx_r8_cae975'

def setup_inputs(seed: int=0):
    np.random.seed(seed)
    _w = jnp.asarray

    def _rec_inputs():
        import jax
        import jax.numpy as jnp
        _rk = jax.random.key(seed)
        x = -0.0003929 + 0.9999 * jax.random.normal(jax.random.fold_in(_rk, 1), (16, 64, 512), jnp.float32)
        _lenS = 64 - jax.random.randint(jax.random.fold_in(_rk, 7), (16,), 0, max(1, 64 // 4) + 1, jnp.int32)
        _lenS2 = 64 - jax.random.randint(jax.random.fold_in(_rk, 8), (16,), 0, max(1, 64 // 4) + 1, jnp.int32)
        _ctx_4096P = jax.random.normal(jax.random.fold_in(_rk, 11), (16, 16, 512), jnp.float32)
        _ctx_4096c = jax.random.dirichlet(jax.random.fold_in(_rk, 511), 0.3 * jnp.ones((16,), jnp.float32), (16, 64))
        _ctx_4096t = jnp.einsum('bsk,bkd->bsd', _ctx_4096c, _ctx_4096P)
        _ctx_4096t = _ctx_4096t * jax.lax.rsqrt(jnp.mean(jnp.square(_ctx_4096t)) + 1e-12) * 0.953939
        ctx_4096 = 2.81802e-05 + 1.00001 * (_ctx_4096t + 0.3 * jax.random.normal(jax.random.fold_in(_rk, 611), (16, 64, 512), jnp.float32))
        pos_BxS2 = jnp.broadcast_to(jnp.arange(64, dtype=jnp.int32), (16, 64))
        _validS = jnp.arange(64)[None, :] < _lenS[:, None]
        _validS2 = jnp.arange(64)[None, :] < _lenS2[:, None]
        _causal = jnp.tril(jnp.ones((64, 64), dtype=bool))
        mask_BxSxS2_ik0 = jnp.where(jnp.broadcast_to(_validS2[:, None, :], (16, 64, 64)), 0, 1).astype(jnp.int32)
        return (x, ctx_4096, pos_BxS2, mask_BxSxS2_ik0)
    x, ctx_4096, pos_BxS2, mask_BxSxS2_ik0 = _rec_inputs()

    def _L0_attn_setup():
        import jax, jax.numpy as jnp
        import numpy as np
        BH = 32
        BW = 32
        key = jax.random.key(seed)
        k1, k2, k3, k4 = jax.random.split(key, 4)
        B, S, K, N = (2, 256, 512, 512)
        data = jax.random.normal(k1, (B, S, K), dtype=jnp.float32)
        weight = jax.random.normal(k2, (N, K), dtype=jnp.float32) * 0.02
        bias = jax.random.normal(k3, (N,), dtype=jnp.float32) * 0.02
        Nb, Kb = (N // BH, K // BW)
        block_on = jax.random.uniform(k4, (Nb, Kb)) < 0.3
        mask = jnp.repeat(jnp.repeat(block_on, BH, axis=0), BW, axis=1).astype(jnp.int32)
        return {'data': data, 'mask': mask, 'weight': weight, 'bias': bias}
    _L0_attn_all = _L0_attn_setup()
    _L0_attn_in = {k: v for k, v in _L0_attn_all.items() if k in ('mask', 'weight', 'bias')}
    del _L0_attn_all

    def _L0_xattn_setup():
        import jax, jax.numpy as jnp
        import numpy as np
        B, S, E = (2, 256, 512)
        H, KVH, D = (32, 8, 128)
        GROUPS = H // KVH
        MAX_POS = 512
        ROPE_THETA = 10000.0

        def _rope_tables(max_pos, dim, theta):
            inv_freq = 1.0 / theta ** (jnp.arange(0, dim, 2, dtype=jnp.float32) / dim)
            t = jnp.arange(max_pos, dtype=jnp.float32)
            freqs = jnp.einsum('i,j->ij', t, inv_freq)
            emb = jnp.concatenate([freqs, freqs], axis=-1)
            return (jnp.cos(emb), jnp.sin(emb))

        def _rotate_half(x):
            x1, x2 = (x[..., :x.shape[-1] // 2], x[..., x.shape[-1] // 2:])
            return jnp.concatenate([-x2, x1], axis=-1)
        key = jax.random.key(seed)
        ks = jax.random.split(key, 8)
        scale_w = 1.0 / np.sqrt(E)
        query = jax.random.normal(ks[0], (B, S, E), dtype=jnp.float32)
        k_in = jax.random.normal(ks[1], (B, S, E), dtype=jnp.float32)
        v_in = jax.random.normal(ks[2], (B, S, E), dtype=jnp.float32)
        position_ids = jnp.broadcast_to(jnp.arange(S, dtype=jnp.int64), (B, S))
        src_mask = jnp.tril(jnp.ones((S, S), dtype=jnp.int32))
        src_mask = jnp.broadcast_to(src_mask, (B, S, S))
        Wq = jax.random.normal(ks[3], (E, H * D), dtype=jnp.float32) * scale_w
        Wk = jax.random.normal(ks[4], (E, KVH * D), dtype=jnp.float32) * scale_w
        Wv = jax.random.normal(ks[5], (E, KVH * D), dtype=jnp.float32) * scale_w
        Wo = jax.random.normal(ks[6], (H * D, E), dtype=jnp.float32) * scale_w
        return {'query': query, 'key': k_in, 'value': v_in, 'position_ids': position_ids, 'src_mask': src_mask, 'Wq': Wq, 'Wk': Wk, 'Wv': Wv, 'Wo': Wo}
    _L0_xattn_all = _L0_xattn_setup()
    _L0_xattn_in = {k: v for k, v in _L0_xattn_all.items() if k in ('Wq', 'Wk', 'Wv', 'Wo')}
    del _L0_xattn_all

    def _L0_ffn_setup():
        import jax, jax.numpy as jnp
        import numpy as np
        LORA_R = 16
        SCALE = 16.0 / np.sqrt(16.0)
        NUM_EXPERTS = 4
        TOP_K = 2
        IN_F = 512
        OUT_F = 512
        key = jax.random.key(seed)
        k_x, k_a, k_b, k_r = jax.random.split(key, 4)
        x = jax.random.normal(k_x, (2, 256, IN_F), dtype=jnp.float32)
        A = jax.random.normal(k_a, (NUM_EXPERTS, LORA_R, IN_F), dtype=jnp.float32) * (1.0 / np.sqrt(IN_F))
        B = jax.random.normal(k_b, (NUM_EXPERTS, OUT_F, LORA_R), dtype=jnp.float32) * 0.02
        Wr = jax.random.normal(k_r, (NUM_EXPERTS, IN_F), dtype=jnp.float32) * 0.02
        return {'x': x, 'A': A, 'B': B, 'Wr': Wr}
    _L0_ffn_all = _L0_ffn_setup()
    _L0_ffn_in = {k: v for k, v in _L0_ffn_all.items() if k in ('A', 'B', 'Wr')}
    del _L0_ffn_all
    return {'x': x, 'ctx_4096': ctx_4096, 'pos_BxS2': pos_BxS2, 'mask_BxSxS2_ik0': mask_BxSxS2_ik0, 'L0_attn_mask': _L0_attn_in['mask'], 'L0_attn_weight': _L0_attn_in['weight'], 'L0_attn_bias': _L0_attn_in['bias'], 'L0_xattn_Wq': _L0_xattn_in['Wq'], 'L0_xattn_Wk': _L0_xattn_in['Wk'], 'L0_xattn_Wv': _L0_xattn_in['Wv'], 'L0_xattn_Wo': _L0_xattn_in['Wo'], 'L0_ffn_A': _L0_ffn_in['A'], 'L0_ffn_B': _L0_ffn_in['B'], 'L0_ffn_Wr': _L0_ffn_in['Wr']}

def reference(x, ctx_4096, pos_BxS2, mask_BxSxS2_ik0, L0_attn_mask, L0_attn_weight, L0_attn_bias, L0_xattn_Wq, L0_xattn_Wk, L0_xattn_Wv, L0_xattn_Wo, L0_ffn_A, L0_ffn_B, L0_ffn_Wr):
    import jax
    import jax.numpy as jnp

    def _L0_attn_ref(data, mask, weight, bias):
        import jax, jax.numpy as jnp
        import numpy as np
        BH = 32
        BW = 32
        N, K = weight.shape
        Nb, Kb = (N // BH, K // BW)
        bm = mask.reshape(Nb, BH, Kb, BW).sum(axis=(1, 3)) > 0
        wb = weight.reshape(Nb, BH, Kb, BW) * bm[:, None, :, None].astype(weight.dtype)
        w = wb.reshape(N, K)
        out = jnp.einsum('bsk,nk->bsn', data, w) + bias
        return out

    def _L0_xattn_ref(query, key, value, position_ids, src_mask, Wq, Wk, Wv, Wo):
        import jax, jax.numpy as jnp
        import numpy as np
        B, S, E = (2, 256, 512)
        H, KVH, D = (32, 8, 128)
        GROUPS = H // KVH
        MAX_POS = 512
        ROPE_THETA = 10000.0

        def _rope_tables(max_pos, dim, theta):
            inv_freq = 1.0 / theta ** (jnp.arange(0, dim, 2, dtype=jnp.float32) / dim)
            t = jnp.arange(max_pos, dtype=jnp.float32)
            freqs = jnp.einsum('i,j->ij', t, inv_freq)
            emb = jnp.concatenate([freqs, freqs], axis=-1)
            return (jnp.cos(emb), jnp.sin(emb))

        def _rotate_half(x):
            x1, x2 = (x[..., :x.shape[-1] // 2], x[..., x.shape[-1] // 2:])
            return jnp.concatenate([-x2, x1], axis=-1)
        nb, q_len, _ = query.shape
        q = (query @ Wq).reshape(nb, q_len, H, D).transpose(0, 2, 1, 3)
        k = (key @ Wk).reshape(nb, q_len, KVH, D).transpose(0, 2, 1, 3)
        v = (value @ Wv).reshape(nb, q_len, KVH, D).transpose(0, 2, 1, 3)
        cos_t, sin_t = _rope_tables(MAX_POS, D, ROPE_THETA)
        cos = cos_t[position_ids][:, None]
        sin = sin_t[position_ids][:, None]
        q = q * cos + _rotate_half(q) * sin
        k = k * cos + _rotate_half(k) * sin
        k = jnp.repeat(k, GROUPS, axis=1)
        v = jnp.repeat(v, GROUPS, axis=1)
        scores = jnp.einsum('bhqd,bhkd->bhqk', q, k) / jnp.sqrt(jnp.float32(D))
        mask = src_mask[:, None]
        scores = jnp.where(mask == 0, jnp.float32(-1000000000.0), scores)
        attn = jax.nn.softmax(scores, axis=-1)
        x = jnp.einsum('bhqk,bhkd->bhqd', attn, v)
        x = x.transpose(0, 2, 1, 3).reshape(nb, q_len, H * D)
        return x @ Wo

    def _L0_ffn_ref(x, A, B, Wr):
        import jax, jax.numpy as jnp
        import numpy as np
        LORA_R = 16
        SCALE = 16.0 / np.sqrt(16.0)
        NUM_EXPERTS = 4
        TOP_K = 2
        IN_F = 512
        OUT_F = 512
        orig_shape = x.shape
        flat = x.reshape(-1, orig_shape[-1])
        logits = flat @ Wr.T
        topk_vals, topk_idx = jax.lax.top_k(logits, TOP_K)
        T = flat.shape[0]
        neg_inf = jnp.finfo(logits.dtype).min
        sparse = jnp.full_like(logits, neg_inf)
        rows = jnp.arange(T)[:, None]
        sparse = sparse.at[rows, topk_idx].set(topk_vals)
        gates = jax.nn.softmax(sparse, axis=-1)
        mid = jnp.einsum('tf,erf->ter', flat, A)
        all_deltas = jnp.einsum('ter,eor->teo', mid, B) * SCALE
        delta = jnp.sum(gates[:, :, None] * all_deltas, axis=1)
        return delta.reshape(*orig_shape[:-1], -1)
    x = x + _L0_attn_ref(_layernorm(x, axis=-1), L0_attn_mask, L0_attn_weight, L0_attn_bias)
    x = x + _L0_xattn_ref(_layernorm(x, axis=-1), ctx_4096, ctx_4096, pos_BxS2, mask_BxSxS2_ik0, L0_xattn_Wq, L0_xattn_Wk, L0_xattn_Wv, L0_xattn_Wo)
    x = x + _L0_ffn_ref(_layernorm(x, axis=-1), L0_ffn_A, L0_ffn_B, L0_ffn_Wr)
    return x

_drawn_inputs = setup_inputs


def setup_inputs(seed=0):
    import zlib

    import numpy as np

    out = dict(_drawn_inputs(seed))
    spreads = {}
    factors = {'L0_attn_bias': 4.202}
    for name, (base, spread) in spreads.items():
        noise = np.random.default_rng([zlib.crc32(name.encode()), seed]).standard_normal(out[name].shape)
        drawn = base * np.exp(spread * noise) if base else spread * noise
        out[name] = jnp.asarray(drawn.astype(out[name].dtype))
    for name, factor in factors.items():
        out[name] = (out[name] * factor).astype(out[name].dtype)
    return out
```

```python
from contextlib import ExitStack

import numpy as np

import concourse.bass as bass
from concourse import mybir

F32 = mybir.dt.float32
F32R = mybir.dt.float32r
I32 = mybir.dt.int32
ALU = mybir.AluOpType
ACT = mybir.ActivationFunctionType
AX = mybir.AxisListType

P = 128
HALF = P // 2
BANK = 512
HEADS, KV_HEADS, HEAD_DIM = 32, 8, 128
GROUP = HEADS // KV_HEADS
MAX_POS = 512
THETA = 10000.0
SPARSE_BLOCK = 32
EXPERTS, RANK = 4, 16
ER = EXPERTS * RANK
LORA_SCALE = 16.0 / 4.0
EPS = 1e-5
MASK_FILL = -1e9 * float(np.sqrt(HEAD_DIM))
NO_CAP = 3.0e38

C_IDENT = 0
C_BLOCKS = C_IDENT + P
C_TABLE = C_BLOCKS + P
C_IOTA = C_TABLE + MAX_POS // P * P
C_TRIL = C_IOTA + MAX_POS // P
C_END = C_TRIL + EXPERTS * EXPERTS


def shape_constants():
    c = np.zeros((P, C_END), np.float32)
    c[:, C_IDENT:C_BLOCKS] = np.eye(P, dtype=np.float32)
    n = np.arange(P)
    c[:, C_BLOCKS:C_TABLE] = n[:, None] // SPARSE_BLOCK == n[None, :] // SPARSE_BLOCK
    exponent = np.arange(0, HEAD_DIM, 2, dtype=np.float32) / np.float32(HEAD_DIM)
    inv_freq = (np.float32(1.0) / np.power(np.float32(THETA), exponent)).astype(np.float32)
    angle = np.arange(MAX_POS, dtype=np.float32)[:, None] * inv_freq[None, :]
    table = np.concatenate([np.cos(angle), np.sin(angle)], axis=1).astype(np.float32)
    c[:, C_TABLE:C_IOTA] = table.reshape(MAX_POS // P, P, P).transpose(1, 0, 2).reshape(P, -1)
    c[:, C_IOTA:C_TRIL] = n[:, None] + P * np.arange(MAX_POS // P)[None, :]
    c[:, C_TRIL:C_END] = np.tril(np.ones((EXPERTS, EXPERTS), np.float32), -1).reshape(1, -1)
    return c


def decoder_layer(nc, x, ctx_in, pos, smask, w_mask, w_attn, bias, wq, wk, wv, wo, lora_a, lora_b, w_router,
                  consts, out):
    B, S, E = x.shape
    TOK = B * S
    TILES = TOK // P
    CH = E // P
    UTOK = BANK
    UTILES = UTOK // P
    UB = UTOK // S
    PAIRS = KV_HEADS // 2
    PW = 2 * HEAD_DIM
    HW = GROUP * HEAD_DIM
    UNITS = TOK // UTOK
    assert (B, S, E, UNITS, CH, GROUP) == (16, 64, 512, 2, 4, 4)
    SCORE_SCALE = 1.0 / float(np.sqrt(HEAD_DIM))

    x_rows = x.rearrange("b s e -> (b s) e")
    ctx_rows = ctx_in.rearrange("b s e -> (b s) e")
    out_rows = out.rearrange("b s e -> (b s) e")
    pos_row = pos.rearrange("b s -> (b s)")
    v_dram = nc.dram_tensor("v_scratch", (KV_HEADS, P, TILES, HEAD_DIM), F32, kind="Internal").ap()

    with ExitStack() as stack:
        def sb(name, shape, dt=F32):
            return stack.enter_context(nc.sbuf_tensor(name, shape, dt))

        def sem(name):
            return stack.enter_context(nc.semaphore(name))

        bank = [stack.enter_context(nc.psum_tensor(f"bank{i}", [P, BANK], F32)) for i in range(8)]
        QK, SC, TR, WO = bank[0:2], bank[2:4], bank[4:6], bank[6:8]

        con = sb("con", [P, C_END])
        ident = con[:, C_IDENT:C_BLOCKS]
        xnT_hi = sb("xnT_hi", [P, CH, TOK], F32R)
        xnT_lo = sb("xnT_lo", [P, CH, TOK], F32R)
        xacc = sb("xacc", [P, TILES, E])
        cosT = sb("cosT", [P, TOK])
        sinT = sb("sinT", [P, TOK])
        cap = sb("cap", [P, B, S])

        wide_hi = sb("wide_hi", [P, CH, TOK], F32R)
        wide_lo = sb("wide_lo", [P, CH, TOK], F32R)
        ctxT_hi, ctxT_lo = wide_hi, wide_lo
        wq_hi, wo_hi = wide_hi[:, 0:CH // 2, :], wide_hi[:, CH // 2:CH, :]
        wq_lo, wo_lo = wide_lo[:, 0:CH // 2, :], wide_lo[:, CH // 2:CH, :]
        wq_hi, wq_lo, wo_hi, wo_lo = (v.rearrange("p a (b n) -> p (a b) n", n=HW) for v in (wq_hi, wq_lo, wo_hi, wo_lo))

        mid_hi = sb("mid_hi", [P, GROUP * UTOK], F32R)
        mid_lo = sb("mid_lo", [P, GROUP * UTOK], F32R)
        half = CH * PW
        wk_hi, wk_lo = (m[:, 0:half].rearrange("p (c n) -> p c n", c=CH) for m in (mid_hi, mid_lo))
        wv_hi, wv_lo = (m[:, half:2 * half].rearrange("p (c n) -> p c n", c=CH) for m in (mid_hi, mid_lo))
        oT_hi, oT_lo = (m[:, :].rearrange("p (h t) -> p h t", h=GROUP) for m in (mid_hi, mid_lo))

        raw = sb("raw", [P, TILES, E])
        wq_raw, wo_raw = raw[:, 0:CH, :], raw[:, CH:2 * CH, :]

        q_mem = sb("q_mem", [P, GROUP * UTOK])
        wk_raw = q_mem[:, 0:CH * PW].rearrange("p (c n) -> p c n", c=CH)
        wv_raw = q_mem[:, CH * PW:2 * CH * PW].rearrange("p (c n) -> p c n", c=CH)
        q_rot = q_mem[:, :].rearrange("p (hp b h q) -> p hp b h q", hp=2, b=UB, h=2)

        k_rot = sb("k_rot", [P, KV_HEADS, TOK])
        onehot = k_rot[:, 0:4, :]
        w_rows = k_rot[:, 4:6, :].rearrange("p a (b n) -> p (a b) n", n=E)
        m_rows = k_rot[:, 6:8, :].rearrange("p a (b n) -> p (a b) n", n=E)
        ffn = k_rot[:, 0:6, :].rearrange("p a (b n) -> p (a b) n", n=E)
        ffn_norm, ffn_xT, ffn_out = ffn[:, 0:4, :], ffn[:, 4:8, :], ffn[:, 8:12, :]

        rope_tmp = sb("rope_tmp", [P, 4, UTOK])
        swapped, cos_part = rope_tmp[:, 0:2, :], rope_tmp[:, 2:4, :]
        pos_f = rope_tmp[:, 0:2, :].rearrange("p a b -> p (a b)")
        pos_i = rope_tmp[:, 2:4, :].rearrange("p a b -> p (a b)")

        soft = sb("soft", [P, 4, BANK])
        v_stage = soft
        shifted, probs = soft[:, 0:2, :], soft[:, 2:4, :]
        ar_rows = soft[0:ER + EXPERTS, 0, :]
        b_rows = soft[:, 1, 0:CH * ER].rearrange("p (c r) -> p c r", c=CH)

        late = sb("late", [P, CH, E])
        wT = late
        v_head = late[:, 0:2, :].rearrange("p a (t d) -> p (a t) d", d=HEAD_DIM)
        pT = late[:, 2:4, :]

        norm = sb("norm", [P, 2, E])
        xn1T = sb("xn1T", [P, 2, E])
        bias_bc = sb("bias_bc", [P, E])
        arT = sb("arT", [P, CH, ER + EXPERTS])
        bT = sb("bT", [ER, E])
        gmT = norm[0:ER, 0, :]
        stats = sb("stats", [P, 2, 6])
        mean_var = sb("mean_var", [P, 2, 2])
        var_eps = sb("var_eps", [P, 2, 1])
        rstd = sb("rstd", [P, 2, 1])
        minus_half = sb("minus_half", [P, 1])
        tick = sb("tick", [P, 1])
        block_sum = sb("block_sum", [P, CH, E // SPARSE_BLOCK])
        block_on = sb("block_on", [P, CH, E // SPARSE_BLOCK])
        row_max = sb("row_max", [P, 2, UB])
        row_sum = sb("row_sum", [P, 2, UB])
        row_inv = sb("row_inv", [P, 2, UB])
        mg = k_rot[:, 6, 0:UTILES * (ER + EXPERTS)].rearrange("p (i n) -> p i n", i=UTILES)
        cmp_gt = sb("cmp_gt", [P, UTILES, EXPERTS, EXPERTS])
        cmp_eq = sb("cmp_eq", [P, UTILES, EXPERTS, EXPERTS])
        g_rank = sb("g_rank", [P, UTILES, EXPERTS])
        g_exp = sb("g_exp", [P, UTILES, EXPERTS])
        g_sel = sb("g_sel", [P, UTILES, EXPERTS])
        g_max = sb("g_max", [P, UTILES])
        g_sum = sb("g_sum", [P, UTILES])
        g_inv = sb("g_inv", [P, UTILES])
        gated = k_rot[:, 6, BANK:BANK + UTILES * ER].rearrange("p (i n) -> p i n", i=UTILES)

        d_con, d_pos, d_mask, d_w, d_bias, d_cap, d_small = (sem(n) for n in (
            "d_con", "d_pos", "d_mask", "d_w", "d_bias", "d_cap", "d_small"))
        d_ctx = [sem(f"d_ctx{i}") for i in range(TILES)]
        d_x = [sem(f"d_x{i}") for i in range(TILES)]
        d_wk, d_wv, d_wq, d_wo, d_v = (sem(n) for n in ("d_wk", "d_wv", "d_wq", "d_wo", "d_v"))
        d_vstore = [sem(f"d_vstore{i}") for i in range(4)]
        d_out = sem("d_out")
        qk_filled, qk_act, qk_dve = sem("qk_filled"), sem("qk_act"), sem("qk_dve")
        sc_filled, sc_act = sem("sc_filled"), sem("sc_act")
        tr_filled, tr_act, tr_dve = sem("tr_filled"), sem("tr_act"), sem("tr_dve")
        wo_filled, x_added = sem("wo_filled"), sem("x_added")
        scores_ready, pT_ready, pT_copied = sem("scores_ready"), sem("pT_ready"), sem("pT_copied")
        o_filled, o_hi, o_lo = sem("o_filled"), sem("o_hi"), sem("o_lo")
        wk_hi_done, wk_split, wv_hi_done, wv_split = (sem(n) for n in ("wk_hi_done", "wk_split", "wv_hi_done", "wv_split"))
        wq_hi_done, wq_split, wo_hi_done, wo_split = (sem(n) for n in ("wq_hi_done", "wq_split", "wo_hi_done", "wo_split"))
        pos_step, hot_done, const_set, cap_step = sem("pos_step"), sem("hot_done"), sem("const_set"), sem("cap_step")
        blocks_reduced, blocks_flagged, w_masked = sem("blocks_reduced"), sem("blocks_flagged"), sem("w_masked")
        ln_stats, ln_aggr, ln_var, ln_rstd, ln_out = (sem(n) for n in ("ln_stats", "ln_aggr", "ln_var", "ln_rstd", "ln_out"))
        biased = sem("biased")
        rope_sin, rotated = sem("rope_sin"), sem("rotated")
        capped, maxed, shift_done, exp_done, summed, inverted, probs_ready = (sem(n) for n in (
            "capped", "maxed", "shift_done", "exp_done", "summed", "inverted", "probs_ready"))
        f_mg, f_mg_copied, f_step, f_tail, f_exp, f_gated, f_gT, f_gT_copied, f_y, f_out = (sem(n) for n in (
            "f_mg", "f_mg_copied", "f_step", "f_tail", "f_exp", "f_gated", "f_gT", "f_gT_copied", "f_y", "f_out"))

        TR_W = TILES
        TR_AR = TR_W + CH
        TR_B = TR_AR + 1
        TR_SETUP = TR_B + 1
        TR_STAGE1 = TR_SETUP + 4 * PAIRS
        QK_K = UNITS
        QK_Q = QK_K + KV_HEADS * UNITS
        SC_V = 1
        ADDED_1 = TILES

        def o_bank(b):
            return b[:, :].rearrange("p (i h q) -> p i h q", i=2, h=GROUP)

        def o_view(m, r, par):
            v = m.rearrange("p h (r i par q) -> p r par i h q", r=2, i=2, par=2)
            return v[:, r, par]

        block = stack.enter_context(nc.Block())

        @block.sync
        def _(sp):
            def load_tiles(n):
                sp.dma_start(raw[:, n, :], ctx_rows[n * P:(n + 1) * P, :]).then_inc(d_ctx[n], 16)

            def load_pair(dst, src, p, done):
                sp.dma_start(dst, src.rearrange("(c k) n -> k c n", k=P)[:, :, bass.ds(p * PW, PW)]).then_inc(done, 16)

            sp.dma_start(con[:, :], consts).then_inc(d_con, 16)
            load_tiles(0)
            load_tiles(1)
            sp.dma_start(m_rows.bitcast(I32), w_mask.rearrange("(c p) k -> p c k", p=P)).then_inc(d_mask, 16)
            sp.dma_start(pos_i.bitcast(I32), pos_row.unsqueeze(0).broadcast_to([P, TOK])).then_inc(d_pos, 16)
            for n in range(2, TILES):
                load_tiles(n)
            sp.dma_start(w_rows, w_attn.rearrange("(c p) k -> p c k", p=P)).then_inc(d_w, 16)
            load_pair(wv_raw, wv, 0, d_wv)
            load_pair(wk_raw, wk, 0, d_wk)
            for n in range(TILES):
                sp.dma_start(xacc[:, n, :], x_rows[n * P:(n + 1) * P, :]).then_inc(d_x[n], 16)
                if n == 1:
                    sp.dma_start(bias_bc[:, :], bias.unsqueeze(0).broadcast_to([P, E])).then_inc(d_bias, 16)
                    sp.dma_start(ar_rows[0:ER, :], lora_a.rearrange("e r k -> (e r) k")).then_inc(d_small, 16)
                    sp.dma_start(ar_rows[ER:ER + EXPERTS, :], w_router).then_inc(d_small, 16)
                    for c in range(CH):
                        sp.dma_start(b_rows[:, c, :].rearrange("p (e r) -> p e r", e=EXPERTS),
                                     lora_b[:, c * P:(c + 1) * P, :].rearrange("e p r -> p e r")).then_inc(d_small, 16)
            for h in range(2):
                sp.dma_start(cap[h * HALF:(h + 1) * HALF, :, :].bitcast(I32),
                             smask.rearrange("b q k -> q b k")).then_inc(d_cap, 16)
            sp.wait_ge(tr_filled, TILES)
            sp.dma_start(wq_raw, wq.rearrange("(c k) n -> k c n", k=P)[:, :, 0:HW]).then_inc(d_wq, 16)
            sp.dma_start(wo_raw, wo[0:HW, :].rearrange("(h d) n -> d h n", d=P)).then_inc(d_wo, 16)

            def stage1(p, last):
                def store_v(v):
                    sp.wait_ge(sc_act, SC_V + 4 * p + v + 1)
                    for g in range(2):
                        sp.dma_start(
                            v_dram[bass.ds(2 * p + g, 1), :, 2 * v:2 * v + 2, :].rearrange("o p t d -> p (o t) d"),
                            v_stage[:, v, :].rearrange("p (t g d) -> p t g d", t=2, g=2)[:, :, g, :],
                        ).then_inc(d_vstore[v], 16)

                if not last:
                    sp.wait_ge(wv_split, p + 1)
                    load_pair(wv_raw, wv, p + 1, d_wv)
                store_v(0)
                store_v(1)
                if not last:
                    sp.wait_ge(wk_split, p + 1)
                    load_pair(wk_raw, wk, p + 1, d_wk)
                store_v(2)
                store_v(3)

            with sp.Fori(0, PAIRS - 1) as p:
                stage1(p, False)
            stage1(PAIRS - 1, True)

            for v in range(4):
                sp.wait_ge(d_vstore[v], 32 * PAIRS)
            sp.wait_ge(wo_filled, TILES)

            def stage2(g, first, last):
                if not first:
                    sp.wait_ge(o_filled, 4 * g)
                sp.dma_start(v_head, v_dram[bass.ds(g, 1)].rearrange("o p t d -> p (o t) d")).then_inc(d_v, 16)
                if not last:
                    sp.wait_ge(wq_split, CH * (g + 1))
                    sp.dma_start(wq_raw, wq.rearrange("(c k) n -> k c n", k=P)[:, :, bass.ds((g + 1) * HW, HW)]
                                 ).then_inc(d_wq, 16)
                    sp.wait_ge(wo_split, GROUP * (g + 1))
                    sp.dma_start(wo_raw, wo[bass.ds((g + 1) * HW, HW), :].rearrange("(h d) n -> d h n", d=P)
                                 ).then_inc(d_wo, 16)

            stage2(0, True, False)
            with sp.Fori(1, KV_HEADS - 1) as g:
                stage2(g, False, False)
            stage2(KV_HEADS - 1, False, True)

            for n in range(TILES):
                sp.wait_ge(f_out, n + 1)
                sp.dma_start(out_rows[n * P:(n + 1) * P, :], ffn_out[:, n % UTILES, :]).then_inc(d_out, 16)
            sp.wait_ge(d_out, 16 * TILES)

        @block.tensor
        def _(pe):
            def mm3(dst, lhs, rhs, first, last):
                pe.matmul(dst, lhs[0], rhs[0], start=first, stop=False)
                pe.matmul(dst, lhs[0], rhs[1], start=False, stop=False)
                return pe.matmul(dst, lhs[1], rhs[0], start=False, stop=last)

            def transpose_tile(dst, rows, n=CH):
                for c in range(n):
                    t = pe.transpose(dst[:, c * P:(c + 1) * P], rows[:, c * P:(c + 1) * P], ident)
                return t

            pe.wait_ge(d_con, 16)
            for n in range(TILES):
                pe.wait_ge(d_ctx[n], 16)
                if n >= 2:
                    pe.wait_ge(tr_act, n - 1)
                    pe.wait_ge(tr_dve, n - 1)
                transpose_tile(TR[n % 2], raw[:, n, :]).then_inc(tr_filled, 1)
            pe.wait_ge(blocks_reduced, 1)
            pe.matmul(SC[0][:, 0:CH * (E // SPARSE_BLOCK)], con[:, C_BLOCKS:C_TABLE],
                      block_sum[:, :, :].rearrange("p c b -> p (c b)"), start=True, stop=True).then_inc(sc_filled, 1)
            for t in range(UNITS):
                for c in range(MAX_POS // P):
                    pe.wait_ge(hot_done, c + 1)
                    m = pe.matmul(QK[t][:, :], con[:, C_TABLE + c * P:C_TABLE + (c + 1) * P],
                                  onehot[:, c, t * UTOK:(t + 1) * UTOK], start=(c == 0), stop=(c == MAX_POS // P - 1))
                m.then_inc(qk_filled, 1)
            pe.wait_ge(w_masked, 1)
            for c in range(CH):
                n = TR_W + c
                pe.wait_ge(tr_act, n - 1)
                pe.wait_ge(tr_dve, min(n - 1, TILES))
                for r in range(CH):
                    m = pe.transpose(TR[n % 2][:, r * P:(r + 1) * P], w_rows[:, r, c * P:(c + 1) * P], ident)
                m.then_inc(tr_filled, 1)
            pe.wait_ge(d_small, 16 * (2 + CH))
            pe.wait_ge(tr_act, TR_AR - 1)
            for c in range(CH):
                m = pe.transpose(TR[TR_AR % 2][:, c * P:c * P + ER + EXPERTS], ar_rows[:, c * P:(c + 1) * P],
                                 con[0:ER + EXPERTS, 0:ER + EXPERTS])
            m.then_inc(tr_filled, 1)
            pe.wait_ge(tr_act, TR_B - 1)
            for c in range(CH):
                m = pe.transpose(TR[TR_B % 2][0:ER, c * P:(c + 1) * P], b_rows[:, c, :], ident)
            m.then_inc(tr_filled, 1)
            pe.wait_ge(tr_act, TILES)
            pe.wait_ge(tr_dve, TILES)

            def project_v(p, v):
                pe.wait_ge(sc_act, SC_V + 4 * p + v - 1 if v else SC_V + 4 * p)
                for j in range(2):
                    tile = 2 * v + j
                    tok = slice(tile * P, (tile + 1) * P)
                    for c in range(CH):
                        m = mm3(SC[v % 2][:, j * PW:(j + 1) * PW], (ctxT_hi[:, c, tok], ctxT_lo[:, c, tok]),
                                (wv_hi[:, c, :], wv_lo[:, c, :]), c == 0, c == CH - 1)
                m.then_inc(sc_filled, 1)

            def project_k(p, h):
                for t in range(UNITS):
                    m_use = QK_K + 4 * p + 2 * h + t
                    pe.wait_ge(qk_act, m_use - 1)
                    pe.wait_ge(qk_dve, m_use - 1)
                    tok = slice(t * UTOK, (t + 1) * UTOK)
                    col = slice(h * HEAD_DIM, (h + 1) * HEAD_DIM)
                    for c in range(CH):
                        m = mm3(QK[t][:, :], (wk_hi[:, c, col], wk_lo[:, c, col]),
                                (ctxT_hi[:, c, tok], ctxT_lo[:, c, tok]), c == 0, c == CH - 1)
                    m.then_inc(qk_filled, 1)

            def transpose_norm(p, second):
                for j in range(2):
                    use = TR_SETUP + 4 * p + 2 * second + j
                    pe.wait_ge(ln_out, 4 * p + 2 * second + j + 1)
                    pe.wait_ge(tr_act, use - 1)
                    if not second:
                        pe.wait_ge(tr_dve, TILES + 2 * p + j - 1 if j else TILES + 2 * p)
                    transpose_tile(TR[j], norm[:, j, :]).then_inc(tr_filled, 1)

            def linear(p):
                for j in range(2):
                    pe.wait_ge(tr_act, TR_SETUP + 4 * p + j + 1)
                    for c in range(CH):
                        m = pe.matmul(WO[j][:, :], xn1T[:, j, c * P:(c + 1) * P], wT[:, c, :],
                                      start=(c == 0), stop=(c == CH - 1))
                    m.then_inc(wo_filled, 1)

            with pe.Fori(0, PAIRS) as p:
                pe.wait_ge(wv_split, p + 1)
                project_v(p, 0)
                project_v(p, 1)
                transpose_norm(p, 0)
                project_v(p, 2)
                project_v(p, 3)
                linear(p)
                pe.wait_ge(wk_split, p + 1)
                project_k(p, 0)
                transpose_norm(p, 1)
                project_k(p, 1)

            def project_q(u, t, h):
                use = QK_Q + GROUP * u + h
                pe.wait_ge(qk_act, use - 1)
                pe.wait_ge(qk_dve, use - 1)
                tok = slice(t * UTOK, (t + 1) * UTOK)
                col = slice(h * HEAD_DIM, (h + 1) * HEAD_DIM)
                for c in range(CH):
                    if t == 0 and h == 0:
                        pe.wait_ge(wq_split, CH // 2 * u + c + 1)
                    m = mm3(QK[h % 2][:, :], (wq_hi[:, c, col], wq_lo[:, c, col]),
                            (xnT_hi[:, c, tok], xnT_lo[:, c, tok]), c == 0, c == CH - 1)
                m.then_inc(qk_filled, 1)

            def scores(g, u, t):
                for hp in range(2):
                    pe.wait_ge(rotated, KV_HEADS * UNITS + GROUP * u + 2 * hp + 2)
                    for b in range(UB):
                        m = pe.matmul(SC[hp][:, b * S:(b + 1) * S], q_rot[:, hp, b, :, :].rearrange("p h q -> p (h q)"),
                                      k_rot[:, bass.ds(g, 1), t * UTOK + b * S:t * UTOK + (b + 1) * S].rearrange("p o k -> p (o k)"),
                                      start=True, stop=True)
                    m.then_inc(scores_ready, 1)

            def transpose_probs(u):
                for hp in range(2):
                    pe.wait_ge(probs_ready, 2 * u + hp + 1)
                    transpose_tile(SC[hp], probs[:, hp, :]).then_inc(pT_ready, 1)

            def times_v(g, u, t):
                pe.wait_ge(d_v, 16 * g + 16)
                pe.wait_ge(pT_copied, 2 * u + 2)
                for r in range(2):
                    banks = (TR, SC)[r]
                    for i in range(2):
                        for par in range(2):
                            lane = slice(par * HALF, (par + 1) * HALF)
                            bp = 2 * r + i
                            m = pe.matmul(
                                banks[par][:, i * 256:(i + 1) * 256],
                                v_head[lane, t * UTILES + bp, :],
                                pT[lane, :, bp * P:(bp + 1) * P], start=True, stop=True)
                    m.then_inc(o_filled, 1)

            def project_out(g, u):
                pe.wait_ge(wo_split, GROUP * (g + 1))
                for i in range(UTILES):
                    pe.wait_ge(o_hi, 4 * u + 2 * (i // 2) + 2)
                    pe.wait_ge(o_lo, 4 * u + 2 * (i // 2) + 2)
                    pe.wait_ge(x_added, ADDED_1 + UTILES * u + i - 1)
                    tok = slice(i * P, (i + 1) * P)
                    for h in range(GROUP):
                        m = mm3(WO[i % 2][:, :], (oT_hi[:, h, tok], oT_lo[:, h, tok]),
                                (wo_hi[:, h, :], wo_lo[:, h, :]), h == 0, h == GROUP - 1)
                    m.then_inc(wo_filled, 1)

            def unit(g, t, following):
                u = 2 * g + t
                scores(g, u, t)
                if following:
                    for h in range(3):
                        project_q(u + 1, 1 - t, h)
                transpose_probs(u)
                if following:
                    project_q(u + 1, 1 - t, 3)
                times_v(g, u, t)
                project_out(g, u)

            pe.wait_ge(tr_act, TR_STAGE1)
            pe.wait_ge(tr_dve, TILES + TILES)
            for h in range(GROUP):
                project_q(0, 0, h)
            with pe.Fori(0, KV_HEADS - 1) as g:
                unit(g, 0, True)
                unit(g, 1, True)
            unit(KV_HEADS - 1, 0, True)
            unit(KV_HEADS - 1, 1, False)

            def experts(t):
                for i in range(UTILES):
                    use = UTILES * t + i
                    pe.wait_ge(ln_out, 4 * PAIRS + use + 1)
                    if use >= 2:
                        pe.wait_ge(tr_act, TR_STAGE1 + use - 1)
                    transpose_tile(TR[i % 2], ffn_norm[:, i, :]).then_inc(tr_filled, 1)
                for i in range(UTILES):
                    pe.wait_ge(tr_act, TR_STAGE1 + UTILES * t + i + 1)
                    if t:
                        pe.wait_ge(f_mg_copied, t)
                    for c in range(CH):
                        m = pe.matmul(SC[0][:, i * 68:i * 68 + ER + EXPERTS], ffn_xT[:, i, c * P:(c + 1) * P],
                                      arT[:, c, :], start=(c == 0), stop=(c == CH - 1))
                m.then_inc(f_mg, 1)
                pe.wait_ge(f_gated, t + 1)
                for i in range(UTILES):
                    m = pe.transpose(SC[1][0:ER, i * P:(i + 1) * P], gated[:, i, :], ident)
                m.then_inc(f_gT, 1)
                pe.wait_ge(f_gT_copied, t + 1)
                for i in range(UTILES):
                    use = UTILES * t + i
                    if use >= 2:
                        pe.wait_ge(f_out, use - 1)
                    pe.matmul(WO[i % 2][:, :], gmT[:, i * P:(i + 1) * P], bT[:, :], start=True, stop=True).then_inc(f_y, 1)

            for t in range(UNITS):
                experts(t)

        @block.scalar
        def _(act):
            def copy(dst, src):
                return act.activation(dst, src, ACT.Copy)

            def tok_tile(m, n):
                return m[:, :, bass.ds(n * P, P)]

            def bank_chunks(b):
                return b[:, :].rearrange("p (c t) -> p c t", c=CH)

            for n in range(TILES):
                act.wait_ge(tr_filled, n + 1)
                copy(tok_tile(ctxT_hi, n), bank_chunks(TR[n % 2])).then_inc(tr_act, 1)
            act.wait_ge(sc_filled, 1)
            copy(block_on[:, :, :].rearrange("p c b -> p (c b)"), SC[0][:, 0:CH * (E // SPARSE_BLOCK)]).then_inc(sc_act, 1)
            act.wait_ge(d_wv, 16)
            copy(wv_hi, wv_raw).then_inc(wv_hi_done, 1)
            for t in range(UNITS):
                act.wait_ge(qk_filled, t + 1)
                tok = slice(t * UTOK, (t + 1) * UTOK)
                copy(cosT[0:HALF, tok], QK[t][0:HALF, :])
                copy(cosT[HALF:P, tok], QK[t][0:HALF, :]).then_inc(qk_act, 1)
            for c in range(CH):
                act.wait_ge(tr_filled, TR_W + c + 1)
                copy(wT[:, c, :], TR[(TR_W + c) % 2][:, :]).then_inc(tr_act, 1)
            act.wait_ge(tr_filled, TR_AR + 1)
            copy(arT[:, :, :], bank_chunks(TR[TR_AR % 2])[:, :, 0:ER + EXPERTS]).then_inc(tr_act, 1)
            act.wait_ge(tr_filled, TR_B + 1)
            copy(bT[:, :], TR[TR_B % 2][0:ER, :]).then_inc(tr_act, 1)

            def swap_halves(use, b):
                act.wait_ge(qk_filled, use + 1)
                if not isinstance(use, int) or use >= QK_K + 2:
                    act.wait_ge(rotated, use - QK_K - 1)
                copy(swapped[0:HALF, b, :], QK[b][HALF:P, :])
                copy(swapped[HALF:P, b, :], QK[b][0:HALF, :]).then_inc(qk_act, 1)

            def copy_v(p, v):
                act.wait_ge(sc_filled, SC_V + 4 * p + v + 1)
                act.wait_ge(d_vstore[v], 32 * p)
                copy(v_stage[:, v, :], SC[v % 2][:, :]).then_inc(sc_act, 1)

            def stage1(p, last):
                act.wait_ge(d_wk, 16 * p + 16)
                act.wait_ge(qk_filled, QK_K + 4 * p)
                copy(wk_hi, wk_raw).then_inc(wk_hi_done, 1)
                copy_v(p, 0)
                copy_v(p, 1)
                for j in range(2):
                    act.wait_ge(tr_filled, TR_SETUP + 4 * p + j + 1)
                    copy(xn1T[:, j, :], TR[j][:, :]).then_inc(tr_act, 1)
                copy_v(p, 2)
                copy_v(p, 3)
                if not last:
                    act.wait_ge(d_wv, 16 * p + 32)
                    copy(wv_hi, wv_raw).then_inc(wv_hi_done, 1)
                swap_halves(QK_K + 4 * p, 0)
                swap_halves(QK_K + 4 * p + 1, 1)
                for j in range(2):
                    act.wait_ge(tr_filled, TR_SETUP + 4 * p + 2 + j + 1)
                    copy(tok_tile(xnT_hi, 2 * p + j), bank_chunks(TR[j])).then_inc(tr_act, 1)
                swap_halves(QK_K + 4 * p + 2, 0)
                swap_halves(QK_K + 4 * p + 3, 1)

            stage1(0, False)
            with act.Fori(1, PAIRS - 1) as p:
                stage1(p, False)
            stage1(PAIRS - 1, True)

            def round_wq(g):
                act.wait_ge(d_wq, 16 * g + 16)
                act.wait_ge(qk_filled, QK_Q + 2 * GROUP * g)
                for c in range(CH):
                    copy(wq_hi[:, c, :], wq_raw[:, c, :]).then_inc(wq_hi_done, 1)

            def round_wo(g):
                act.wait_ge(d_wo, 16 * g + 16)
                act.wait_ge(wo_filled, TILES * (g + 1))
                for h in range(GROUP):
                    copy(wo_hi[:, h, :], wo_raw[:, h, :]).then_inc(wo_hi_done, 1)

            def swap_q(u, h):
                swap_halves(QK_Q + GROUP * u + h, h % 2)

            def unit(g, t, following):
                u = 2 * g + t
                if t == 0:
                    round_wo(g)
                for hp in range(2):
                    act.wait_ge(shift_done, 2 * u + hp + 1)
                    act.activation(shifted[:, hp, :], shifted[:, hp, :], ACT.Exp, scale=SCORE_SCALE).then_inc(exp_done, 1)
                if following:
                    for h in range(3):
                        swap_q(u + 1, h)
                for hp in range(2):
                    act.wait_ge(pT_ready, 2 * u + hp + 1)
                    copy(pT[:, hp, :], SC[hp][:, :]).then_inc(pT_copied, 1)
                if following:
                    swap_q(u + 1, 3)
                for r in range(2):
                    act.wait_ge(o_filled, 2 * u + r + 1)
                    for par in range(2):
                        copy(o_view(oT_hi, r, par), o_bank((TR, SC)[r][par])).then_inc(o_hi, 1)
                if t == 0 and following and not (isinstance(g, int) and g == KV_HEADS - 1):
                    round_wq(g + 1)

            round_wq(0)
            for h in range(GROUP):
                swap_q(0, h)
            with act.Fori(0, KV_HEADS - 1) as g:
                unit(g, 0, True)
                unit(g, 1, True)
            unit(KV_HEADS - 1, 0, True)
            unit(KV_HEADS - 1, 1, False)

            for t in range(UNITS):
                for i in range(UTILES):
                    act.wait_ge(tr_filled, TR_STAGE1 + UTILES * t + i + 1)
                    copy(ffn_xT[:, i, :], TR[i % 2][:, :]).then_inc(tr_act, 1)
                act.wait_ge(f_step, 8 * t + 7)
                act.activation(g_exp[:, :, :], g_exp[:, :, :], ACT.Exp).then_inc(f_exp, 1)
                act.wait_ge(f_gT, t + 1)
                copy(gmT[:, :], SC[1][0:ER, :]).then_inc(f_gT_copied, 1)

        @block.vector
        def _(dve):
            def tt(dst, a, b, op):
                return dve.tensor_tensor(dst, a, b, op)

            def tok_tile(m, n):
                return m[:, :, bass.ds(n * P, P)]

            def bank_chunks(b):
                return b[:, :].rearrange("p (c t) -> p c t", c=CH)

            def by_batch(a):
                return a.rearrange("p (b k) -> p b k", k=S)

            def carry_wait():
                dve.memset(tick[:, :], 0.0)

            def layernorm_pair(pair, rows, dst):
                n = 2 * pair
                carry_wait()
                for j in range(2):
                    dve.bn_stats(stats[:, j, :], rows(j)).then_inc(ln_stats, 1)
                dve.wait_ge(ln_stats, n + 2)
                carry_wait()
                for j in range(2):
                    dve.bn_aggr(mean_var[:, j, :], stats[:, j, :]).then_inc(ln_aggr, 1)
                for j in range(2):
                    dve.wait_ge(ln_aggr, n + j + 1)
                    dve.tensor_scalar(var_eps[:, j, :], mean_var[:, j, 1:2], EPS, None, ALU.add).then_inc(ln_var, 1)
                for j in range(2):
                    dve.wait_ge(ln_rstd, n + j + 1)
                    dve.tensor_scalar(dst(j), rows(j), mean_var[:, j, 0:1], rstd[:, j, :],
                                      ALU.subtract, ALU.mult).then_inc(ln_out, 1)

            dve.memset(minus_half[:, :], -0.5).then_inc(const_set, 1)
            dve.wait_ge(d_pos, 16)
            dve.tensor_copy(pos_f, pos_i.bitcast(I32)).then_inc(pos_step, 1)
            dve.wait_ge(pos_step, 1)
            dve.tensor_scalar(pos_i, pos_f, 0.0, float(MAX_POS), ALU.is_lt, ALU.mult).then_inc(pos_step, 1)
            dve.wait_ge(pos_step, 2)
            tt(pos_f, pos_f, pos_i, ALU.add).then_inc(pos_step, 1)
            dve.wait_ge(pos_step, 3)
            dve.tensor_scalar(pos_f, pos_f, 0.0, float(MAX_POS - 1), ALU.max, ALU.min).then_inc(pos_step, 1)
            dve.wait_ge(d_con, 16)
            dve.wait_ge(pos_step, 4)
            for c in range(MAX_POS // P):
                dve.tensor_scalar(onehot[:, c, :], pos_f, con[:, C_IOTA + c:C_IOTA + c + 1], None,
                                  ALU.is_equal).then_inc(hot_done, 1)

            def ctx_lo(n):
                dve.wait_ge(tr_act, n + 1)
                tt(tok_tile(ctxT_lo, n), bank_chunks(TR[n % 2]), tok_tile(ctxT_hi, n).bitcast(F32),
                   ALU.subtract).then_inc(tr_dve, 1)

            for n in range(4):
                ctx_lo(n)
            dve.wait_ge(d_mask, 16)
            dve.tensor_reduce(block_sum[:, :, :], m_rows.bitcast(I32).rearrange("p c (b k) -> p c b k", k=SPARSE_BLOCK),
                              AX.X, ALU.add).then_inc(blocks_reduced, 1)
            for n in range(4, TILES):
                ctx_lo(n)
            dve.wait_ge(sc_act, 1)
            dve.tensor_scalar(block_sum[:, :, :], block_on[:, :, :], 0.0, None, ALU.is_gt).then_inc(blocks_flagged, 1)
            dve.wait_ge(blocks_flagged, 1)
            dve.wait_ge(d_w, 16)
            w_blocks = w_rows.rearrange("p c (b k) -> p (c b) k", k=SPARSE_BLOCK)
            tt(w_blocks, w_blocks, block_sum[:, :, :].rearrange("p c b -> p (c b)").unsqueeze(2)
               .broadcast_to([P, CH * (E // SPARSE_BLOCK), SPARSE_BLOCK]), ALU.mult).then_inc(w_masked, 1)
            for t in range(UNITS):
                dve.wait_ge(qk_act, t + 1)
                tok = slice(t * UTOK, (t + 1) * UTOK)
                dve.tensor_scalar(sinT[0:HALF, tok], QK[t][HALF:P, :], -1.0, None, ALU.mult)
                dve.tensor_copy(sinT[HALF:P, tok], QK[t][HALF:P, :]).then_inc(qk_dve, 1)

            def rope(use, b, dst):
                n = use - QK_K
                t = dst[1]
                tok = slice(t * UTOK, (t + 1) * UTOK)
                if not isinstance(n, int) or n >= 2:
                    dve.wait_ge(rotated, n - 1)
                dve.wait_ge(qk_act, use + 1)
                tt(cos_part[:, b, :], QK[b][:, :], cosT[:, tok], ALU.mult).then_inc(qk_dve, 1)
                tt(swapped[:, b, :], swapped[:, b, :], sinT[:, tok], ALU.mult).then_inc(rope_sin, 1)
                dve.wait_ge(rope_sin, n + 1)
                tt(dst[0], by_batch(cos_part[:, b, :]), by_batch(swapped[:, b, :]), ALU.add).then_inc(rotated, 1)

            def rope_k(p, h):
                for t in range(UNITS):
                    dst = k_rot[:, bass.ds(2 * p + h, 1), t * UTOK:(t + 1) * UTOK].rearrange("p o k -> p (o k)")
                    rope(QK_K + 4 * p + 2 * h + t, t, (by_batch(dst), t))

            def stage1(p):
                def rows(j):
                    return xacc[:, bass.ds(2 * p + j, 1), :].rearrange("p o e -> p (o e)")

                dve.wait_ge(tr_filled, TR_SETUP + 4 * p)
                layernorm_pair(2 * p, rows, lambda j: norm[:, j, :])
                for j in range(2):
                    dve.wait_ge(biased, 2 * p + j + 1)
                    dve.wait_ge(wo_filled, 2 * p + j + 1)
                    tt(rows(j), rows(j), WO[j][:, :], ALU.add).then_inc(x_added, 1)
                dve.wait_ge(x_added, 2 * p + 2)
                layernorm_pair(2 * p + 1, rows, lambda j: norm[:, j, :])
                rope_k(p, 0)
                for j in range(2):
                    dve.wait_ge(tr_act, TR_SETUP + 4 * p + 2 + j + 1)
                    tt(tok_tile(xnT_lo, 2 * p + j), bank_chunks(TR[j]), tok_tile(xnT_hi, 2 * p + j).bitcast(F32),
                       ALU.subtract).then_inc(tr_dve, 1)
                rope_k(p, 1)

            for n in range(TILES):
                dve.wait_ge(d_x[n], 16)
            stage1(0)
            with dve.Fori(1, PAIRS) as p:
                stage1(p)

            dve.wait_ge(d_cap, 32)
            dve.tensor_scalar(cap[:, :, :], cap[:, :, :].bitcast(I32), 0.0, NO_CAP, ALU.not_equal, ALU.mult).then_inc(cap_step, 1)
            dve.wait_ge(cap_step, 1)
            dve.tensor_scalar(cap[:, :, :], cap[:, :, :], MASK_FILL, None, ALU.add).then_inc(cap_step, 1)
            dve.wait_ge(cap_step, 2)

            def spread(a):
                return a.unsqueeze(2).broadcast_to([P, UB, S])

            def cap_scores(u, t, hp):
                dve.wait_ge(scores_ready, 2 * u + hp + 1)
                tt(by_batch(shifted[:, hp, :]), by_batch(SC[hp][:, :]), cap[:, t * UB:(t + 1) * UB, :],
                   ALU.min).then_inc(capped, 1)

            def find_max(u, hp):
                dve.wait_ge(capped, 2 * u + hp + 1)
                dve.tensor_reduce(row_max[:, hp, :], by_batch(shifted[:, hp, :]), AX.X, ALU.max).then_inc(maxed, 1)

            def shift(u, hp):
                dve.wait_ge(maxed, 2 * u + hp + 1)
                tt(by_batch(shifted[:, hp, :]), by_batch(shifted[:, hp, :]), spread(row_max[:, hp, :]),
                   ALU.subtract).then_inc(shift_done, 1)

            def normalise(u, hp):
                dve.wait_ge(exp_done, 2 * u + hp + 1)
                dve.tensor_reduce(row_sum[:, hp, :], by_batch(shifted[:, hp, :]), AX.X, ALU.add).then_inc(summed, 1)
                dve.wait_ge(summed, 2 * u + hp + 1)
                dve.reciprocal(row_inv[:, hp, :], row_sum[:, hp, :]).then_inc(inverted, 1)
                dve.wait_ge(inverted, 2 * u + hp + 1)
                tt(by_batch(probs[:, hp, :]), by_batch(shifted[:, hp, :]), spread(row_inv[:, hp, :]),
                   ALU.mult).then_inc(probs_ready, 1)

            def rope_q(u, t, h):
                rope(QK_Q + GROUP * u + h, h % 2, (q_rot[:, h // 2, :, h % 2, :], t))

            def unit(g, t, following):
                u = 2 * g + t
                cap_scores(u, t, 0)
                find_max(u, 0)
                cap_scores(u, t, 1)
                shift(u, 0)
                find_max(u, 1)
                shift(u, 1)
                normalise(u, 0)
                if following:
                    rope_q(u + 1, 1 - t, 0)
                normalise(u, 1)
                if following:
                    for h in range(1, GROUP):
                        rope_q(u + 1, 1 - t, h)
                for r in range(2):
                    for par in range(2):
                        dve.wait_ge(o_hi, 4 * u + 2 * r + par + 1)
                        tt(o_view(oT_lo, r, par), o_bank((TR, SC)[r][par]), o_view(oT_hi, r, par).bitcast(F32),
                           ALU.subtract).then_inc(o_lo, 1)
                for i in range(UTILES):
                    dve.wait_ge(wo_filled, TILES + UTILES * u + i + 1)
                    tt(xacc[:, t * UTILES + i, :], xacc[:, t * UTILES + i, :], WO[i % 2][:, :],
                       ALU.add).then_inc(x_added, 1)

            for v in range(4):
                dve.wait_ge(d_vstore[v], 32 * PAIRS)
            for h in range(GROUP):
                rope_q(0, 0, h)
            with dve.Fori(0, KV_HEADS - 1) as g:
                unit(g, 0, True)
                unit(g, 1, True)
            unit(KV_HEADS - 1, 0, True)
            unit(KV_HEADS - 1, 1, False)

            def experts(t):
                steps = 8 * t

                def grid(a, axis):
                    return a.unsqueeze(axis).broadcast_to([P, UTILES, EXPERTS, EXPERTS])

                dve.wait_ge(x_added, ADDED_1 + TILES * KV_HEADS)
                if t:
                    dve.wait_ge(tr_filled, TR_STAGE1 + UTILES * t)
                for pair in range(2):
                    layernorm_pair(2 * PAIRS + 2 * t + pair, lambda j: xacc[:, UTILES * t + 2 * pair + j, :],
                                   lambda j: ffn_norm[:, 2 * pair + j, :])
                dve.wait_ge(f_mg, t + 1)
                dve.tensor_copy(mg[:, :, :], SC[0][:, 0:UTILES * (ER + EXPERTS)]
                                .rearrange("p (i n) -> p i n", i=UTILES)).then_inc(f_mg_copied, 1)
                dve.wait_ge(f_mg_copied, t + 1)
                logit = mg[:, :, ER:ER + EXPERTS]
                dve.tensor_reduce(g_max[:, :], logit, AX.X, ALU.max).then_inc(f_step, 1)
                tt(cmp_gt[:, :, :, :], grid(logit, 2), grid(logit, 3), ALU.is_gt).then_inc(f_step, 1)
                tt(cmp_eq[:, :, :, :], grid(logit, 2), grid(logit, 3), ALU.is_equal).then_inc(f_step, 1)
                dve.wait_ge(f_step, steps + 3)
                tt(cmp_eq[:, :, :, :], cmp_eq[:, :, :, :],
                   con[:, C_TRIL:C_END].rearrange("p (e f) -> p e f", e=EXPERTS).unsqueeze(1)
                   .broadcast_to([P, UTILES, EXPERTS, EXPERTS]), ALU.mult).then_inc(f_step, 1)
                dve.wait_ge(f_step, steps + 4)
                tt(cmp_gt[:, :, :, :], cmp_gt[:, :, :, :], cmp_eq[:, :, :, :], ALU.add).then_inc(f_step, 1)
                dve.wait_ge(f_step, steps + 5)
                dve.tensor_reduce(g_rank[:, :, :], cmp_gt[:, :, :, :], AX.X, ALU.add).then_inc(f_step, 1)
                tt(g_exp[:, :, :], logit, g_max[:, :].unsqueeze(2).broadcast_to([P, UTILES, EXPERTS]),
                   ALU.subtract).then_inc(f_step, 1)
                dve.wait_ge(f_step, steps + 7)
                dve.tensor_scalar(g_sel[:, :, :], g_rank[:, :, :], 1.5, None, ALU.is_lt).then_inc(f_step, 1)
                dve.wait_ge(f_step, steps + 8)
                dve.wait_ge(f_exp, t + 1)
                tt(g_sel[:, :, :], g_sel[:, :, :], g_exp[:, :, :], ALU.mult).then_inc(f_tail, 1)
                dve.wait_ge(f_tail, 4 * t + 1)
                dve.tensor_reduce(g_sum[:, :], g_sel[:, :, :], AX.X, ALU.add).then_inc(f_tail, 1)
                dve.wait_ge(f_tail, 4 * t + 2)
                dve.reciprocal(g_inv[:, :], g_sum[:, :]).then_inc(f_tail, 1)
                dve.wait_ge(f_tail, 4 * t + 3)
                dve.scalar_tensor_tensor(out=g_sel[:, :, :], in0=g_sel[:, :, :], scalar=LORA_SCALE,
                                         in1=g_inv[:, :].unsqueeze(2).broadcast_to([P, UTILES, EXPERTS]),
                                         op0=ALU.mult, op1=ALU.mult).then_inc(f_tail, 1)
                dve.wait_ge(f_tail, 4 * t + 4)
                tt(gated[:, :, :].rearrange("p i (e r) -> p i e r", e=EXPERTS),
                   mg[:, :, 0:ER].rearrange("p i (e r) -> p i e r", e=EXPERTS),
                   g_sel[:, :, :].unsqueeze(3).broadcast_to([P, UTILES, EXPERTS, RANK]), ALU.mult).then_inc(f_gated, 1)
                for i in range(UTILES):
                    n = UTILES * t + i
                    dve.wait_ge(f_y, n + 1)
                    if t:
                        dve.wait_ge(d_out, 16 * UTILES)
                    tt(ffn_out[:, i, :], xacc[:, n, :], WO[i % 2][:, :], ALU.add).then_inc(f_out, 1)

            for t in range(UNITS):
                experts(t)

        @block.gpsimd
        def _(pool):
            def lo_part(dst_lo, value, hi):
                return pool.tensor_tensor(dst_lo, value, hi.bitcast(F32), ALU.subtract)

            def inverse_std(pair):
                for j in range(2):
                    pool.wait_ge(ln_var, 2 * pair + j + 1)
                    pool.tensor_tensor(rstd[:, j, :], var_eps[:, j, :], minus_half[:, :], ALU.pow).then_inc(ln_rstd, 1)

            pool.wait_ge(const_set, 1)
            pool.wait_ge(wv_hi_done, 1)
            lo_part(wv_lo, wv_raw, wv_hi).then_inc(wv_split, 1)
            pool.wait_ge(d_bias, 16)

            def stage1(p, last):
                inverse_std(2 * p)
                pool.wait_ge(wk_hi_done, p + 1)
                lo_part(wk_lo, wk_raw, wk_hi).then_inc(wk_split, 1)
                for j in range(2):
                    pool.wait_ge(ln_out, 4 * p + j + 1)
                    rows = xacc[:, bass.ds(2 * p + j, 1), :].rearrange("p o e -> p (o e)")
                    pool.tensor_tensor(rows, rows, bias_bc[:, :], ALU.add).then_inc(biased, 1)
                inverse_std(2 * p + 1)
                if not last:
                    pool.wait_ge(wv_hi_done, p + 2)
                    lo_part(wv_lo, wv_raw, wv_hi).then_inc(wv_split, 1)

            with pool.Fori(0, PAIRS - 1) as p:
                stage1(p, False)
            stage1(PAIRS - 1, True)

            def split_wq(g):
                for c in range(CH):
                    pool.wait_ge(wq_hi_done, CH * g + c + 1)
                    lo_part(wq_lo[:, c, :], wq_raw[:, c, :], wq_hi[:, c, :]).then_inc(wq_split, 1)

            def split_wo(g):
                for h in range(GROUP):
                    pool.wait_ge(wo_hi_done, GROUP * g + h + 1)
                    lo_part(wo_lo[:, h, :], wo_raw[:, h, :], wo_hi[:, h, :]).then_inc(wo_split, 1)

            split_wq(0)
            with pool.Fori(0, KV_HEADS - 1) as g:
                split_wo(g)
                split_wq(g + 1)
            split_wo(KV_HEADS - 1)
            for pair in range(2 * UNITS):
                inverse_std(2 * PAIRS + pair)


INPUTS = ["x", "ctx_4096", "pos_BxS2", "mask_BxSxS2_ik0", "L0_attn_mask", "L0_attn_weight", "L0_attn_bias",
          "L0_xattn_Wq", "L0_xattn_Wk", "L0_xattn_Wv", "L0_xattn_Wo", "L0_ffn_A", "L0_ffn_B", "L0_ffn_Wr"]


def kernel(**inputs):
    import concourse.bacc as bacc
    from concourse.bass_utils import run_bass_kernel_spmd

    nc = bacc.Bacc("TRN2", target_bir_lowering=False, num_devices=1)
    arrays, args = {}, []
    for name in INPUTS:
        a = np.ascontiguousarray(inputs[name])
        arrays[f"in_{name}"] = a
        args.append(nc.dram_tensor(f"in_{name}", a.shape, mybir.dt.from_np(a.dtype), kind="ExternalInput").ap())
    arrays["in_constants"] = shape_constants()
    args.append(nc.dram_tensor("in_constants", (P, C_END), F32, kind="ExternalInput").ap())
    out = nc.dram_tensor("out_y", tuple(inputs["x"].shape), F32, kind="ExternalOutput").ap()
    decoder_layer(nc, *args, out)
    result = run_bass_kernel_spmd(nc, [arrays], core_ids=[0])
    return result.results[0]["out_y"]
```

```python
from contextlib import ExitStack

import numpy as np

import concourse.bass as bass
from concourse import mybir

F32 = mybir.dt.float32
F32R = mybir.dt.float32r
I32 = mybir.dt.int32
ALU = mybir.AluOpType
ACT = mybir.ActivationFunctionType
AX = mybir.AxisListType

P = 128
HALF = P // 2
BANK = 512
HEADS, KV_HEADS, HEAD_DIM = 32, 8, 128
GROUP = HEADS // KV_HEADS
MAX_POS = 512
THETA = 10000.0
SPARSE_BLOCK = 32
EXPERTS, RANK = 4, 16
ER = EXPERTS * RANK
LORA_SCALE = 16.0 / 4.0
EPS = 1e-5
MASK_FILL = -1e9 * float(np.sqrt(HEAD_DIM))
NO_CAP = 3.0e38

C_IDENT = 0
C_BLOCKS = C_IDENT + P
C_IOTA = C_BLOCKS + P
C_TRIL = C_IOTA + MAX_POS // P
C_END = C_TRIL + EXPERTS * EXPERTS
C_ALL = C_END + MAX_POS // P * P


def shape_constants():
    c = np.zeros((P, C_ALL), np.float32)
    c[:, C_IDENT:C_BLOCKS] = np.eye(P, dtype=np.float32)
    n = np.arange(P)
    c[:, C_BLOCKS:C_IOTA] = n[:, None] // SPARSE_BLOCK == n[None, :] // SPARSE_BLOCK
    exponent = np.arange(0, HEAD_DIM, 2, dtype=np.float32) / np.float32(HEAD_DIM)
    inv_freq = (np.float32(1.0) / np.power(np.float32(THETA), exponent)).astype(np.float32)
    angle = np.arange(MAX_POS, dtype=np.float32)[:, None] * inv_freq[None, :]
    table = np.concatenate([np.cos(angle), np.sin(angle)], axis=1).astype(np.float32)
    c[:, C_END:C_ALL] = table.reshape(MAX_POS // P, P, P).transpose(1, 0, 2).reshape(P, -1)
    c[:, C_IOTA:C_TRIL] = n[:, None] + P * np.arange(MAX_POS // P)[None, :]
    c[:, C_TRIL:C_END] = np.tril(np.ones((EXPERTS, EXPERTS), np.float32), -1).reshape(1, -1)
    return c


def decoder_layer(nc, x, ctx_in, pos, smask, w_mask, w_attn, bias, wq, wk, wv, wo, lora_a, lora_b, w_router,
                  consts, out):
    B, S, E = x.shape
    TOK = B * S
    TILES = TOK // P
    CH = E // P
    UTOK = BANK
    UTILES = UTOK // P
    UB = UTOK // S
    PAIRS = KV_HEADS // 2
    PW = 2 * HEAD_DIM
    HW = GROUP * HEAD_DIM
    UNITS = TOK // UTOK
    assert (B, S, E, UNITS, CH, GROUP) == (16, 64, 512, 2, 4, 4)
    SCORE_SCALE = 1.0 / float(np.sqrt(HEAD_DIM))

    x_rows = x.rearrange("b s e -> (b s) e")
    ctx_rows = ctx_in.rearrange("b s e -> (b s) e")
    out_rows = out.rearrange("b s e -> (b s) e")
    pos_row = pos.rearrange("b s -> (b s)")
    v_dram = nc.dram_tensor("v_scratch", (2, KV_HEADS, P, TILES, HEAD_DIM), F32, kind="Internal").ap()

    with ExitStack() as stack:
        def sb(name, shape, dt=F32):
            return stack.enter_context(nc.sbuf_tensor(name, shape, dt))

        def sem(name):
            return stack.enter_context(nc.semaphore(name))

        bank = [stack.enter_context(nc.psum_tensor(f"bank{i}", [P, BANK], F32)) for i in range(8)]
        QK, SC, TR, WO = bank[0:2], bank[2:4], bank[4:6], bank[6:8]
        RING = [*QK, *WO]
        CTX_T = [*TR, *QK, *WO, *TR]
        W_T = [*TR, *WO]
        SMALL_T = [WO[0], QK[1]]
        LAST_OUT = [*TR, *SC]
        FFN_X = QK
        FFN_MG = [WO[0], SC[0]]
        FFN_GT = [WO[1], SC[1]]
        FFN_Y = [TR[0], TR[1], WO[0], QK[0], TR[0], SC[0], WO[1], QK[1]]

        con = sb("con", [P, C_END])
        ident = con[:, C_IDENT:C_BLOCKS]
        xnT_hi = sb("xnT_hi", [P, CH, TOK], F32R)
        xnT_lo = sb("xnT_lo", [P, CH, TOK], F32R)
        xacc = sb("xacc", [P, TILES, E])
        cosT = sb("cosT", [P, TOK])
        sinT = sb("sinT", [P, TOK])
        cap = sb("cap", [P, B, S])

        wide_hi = sb("wide_hi", [P, CH, TOK], F32R)
        wide_lo = sb("wide_lo", [P, CH, TOK], F32R)
        ctxT_hi, ctxT_lo = wide_hi, wide_lo
        wq_hi, wo_hi = wide_hi[:, 0:CH // 2, :], wide_hi[:, CH // 2:CH, :]
        wq_lo, wo_lo = wide_lo[:, 0:CH // 2, :], wide_lo[:, CH // 2:CH, :]
        wq_hi, wq_lo, wo_hi, wo_lo = (v.rearrange("p a (b n) -> p (a b) n", n=HW) for v in (wq_hi, wq_lo, wo_hi, wo_lo))

        mid_hi = sb("mid_hi", [P, GROUP * UTOK], F32R)
        mid_lo = sb("mid_lo", [P, GROUP * UTOK], F32R)
        half = CH * PW
        wk_hi, wk_lo = (m[:, 0:half].rearrange("p (c n) -> p c n", c=CH) for m in (mid_hi, mid_lo))
        wv_hi, wv_lo = (m[:, half:2 * half].rearrange("p (c n) -> p c n", c=CH) for m in (mid_hi, mid_lo))
        extra_hi, extra_lo = (m[:, half:half + BANK] for m in (mid_hi, mid_lo))
        oT_hi, oT_lo = (m[:, :].rearrange("p (h t) -> p h t", h=GROUP) for m in (mid_hi, mid_lo))

        raw = sb("raw", [P, TILES, E])
        wq_raw, wo_raw = raw[:, 0:CH, :], raw[:, CH:2 * CH, :]
        norm1, norm2 = raw[:, 0:2, :], raw[:, CH:CH + 2, :]
        bias_bc = raw[:, CH + 2, :]

        q_mem = sb("q_mem", [P, GROUP * UTOK])
        wk_raw = q_mem[:, 0:CH * PW].rearrange("p (c n) -> p c n", c=CH)
        wv_raw = q_mem[:, CH * PW:2 * CH * PW].rearrange("p (c n) -> p c n", c=CH)
        q_rot = q_mem[:, :].rearrange("p (hp b h q) -> p hp b h q", hp=2, b=UB, h=2)

        k_rot = sb("k_rot", [P, KV_HEADS, TOK])
        w_rows = k_rot[:, 4:6, :].rearrange("p a (b n) -> p (a b) n", n=E)
        m_rows = k_rot[:, 6:8, :].rearrange("p a (b n) -> p (a b) n", n=E)
        ffn = k_rot[:, 0:4, :].rearrange("p a (b n) -> p (a b) n", n=E)
        ffn_norm, ffn_xT = ffn[:, 0:UTILES, :], ffn[:, UTILES:2 * UTILES, :]
        gated = k_rot[:, 6, 0:UTILES * ER].rearrange("p (i n) -> p i n", i=UTILES)

        rope_tmp = sb("rope_tmp", [P, 4, UTOK])
        swapped, cos_part = rope_tmp[:, 0:2, :], rope_tmp[:, 2:4, :]
        pos_f = rope_tmp[:, 0:2, :].rearrange("p a b -> p (a b)")
        pos_i = rope_tmp[:, 2:4, :].rearrange("p a b -> p (a b)").bitcast(I32)

        gm_split = xnT_hi[:, 0, 0:UTOK]
        b_twice, b_low = xnT_hi[:, 1, 0:E], xnT_lo[0:ER, 0, 0:E]

        onehot = [m[:, :, UTOK:TOK] for m in (xnT_hi, xnT_lo)]

        soft = sb("soft", [P, 4, BANK])
        shifted, probs = soft[:, 0:2, :], soft[:, 2:4, :]
        ar_rows = soft[0:ER + EXPERTS, 2, :]
        b_rows = soft[:, 3, 0:CH * ER].rearrange("p (c r) -> p c r", c=CH)

        late = sb("late", [P, 10 * BANK], F32R)
        wT_hi, wT_lo = (late[:, n * CH * E:(n + 1) * CH * E].rearrange("p (c n) -> p c n", c=CH) for n in range(2))
        table = cap[:, :, :].rearrange("p b k -> p (b k)")[:, 0:BANK]
        xn1T_hi, xn1T_lo = late[:, 8 * BANK:9 * BANK], late[:, 9 * BANK:10 * BANK]
        table_hi, table_lo = xn1T_hi, xn1T_lo
        v_twice = late[:, 0:B * HEAD_DIM].rearrange("p (b d) -> p b d", b=B)
        v_low = late[:, B * HEAD_DIM:(B + TILES) * HEAD_DIM].rearrange("p (t d) -> p t d", t=TILES)
        pT = late[:, 6 * BANK:10 * BANK].rearrange("p (par hp n) -> p par hp n", par=2, hp=2)

        arT = sb("arT", [P, CH, ER + EXPERTS])
        bT = sb("bT", [ER, E])
        stats = sb("stats", [P, 2, 6])
        mean_var = sb("mean_var", [P, 2, 2])
        var_eps = sb("var_eps", [P, 2, 1])
        rstd = sb("rstd", [P, 2, 1])
        minus_half = sb("minus_half", [P, 1])
        tick = sb("tick", [P, 1])
        block_sum = sb("block_sum", [P, CH, E // SPARSE_BLOCK])
        block_on = sb("block_on", [P, CH, E // SPARSE_BLOCK])
        row_max = sb("row_max", [P, 2, UB])
        row_sum = sb("row_sum", [P, 2, UB])
        row_inv = sb("row_inv", [P, 2, UB])
        logit = sb("logit", [P, UTILES, EXPERTS])
        cmp_gt = sb("cmp_gt", [P, UTILES, EXPERTS, EXPERTS])
        cmp_eq = sb("cmp_eq", [P, UTILES, EXPERTS, EXPERTS])
        g_rank = sb("g_rank", [P, UTILES, EXPERTS])
        g_exp = sb("g_exp", [P, UTILES, EXPERTS])
        g_sel = sb("g_sel", [P, UTILES, EXPERTS])
        g_max = sb("g_max", [P, UTILES])
        g_sum = sb("g_sum", [P, UTILES])
        g_inv = sb("g_inv", [P, UTILES])
        g_scale = sb("g_scale", [P, TILES])

        d_ident, d_con, d_pos, d_mask, d_w, d_bias, d_cap, d_small = (sem(n) for n in (
            "d_ident", "d_con", "d_pos", "d_mask", "d_w", "d_bias", "d_cap", "d_small"))
        d_ctx = [sem(f"d_ctx{i}") for i in range(TILES)]
        d_x = [sem(f"d_x{i}") for i in range(TILES)]
        d_wk, d_wv, d_wq, d_wo, d_v = (sem(n) for n in ("d_wk", "d_wv", "d_wq", "d_wo", "d_v"))
        d_vhi = [sem(f"d_vhi{i}") for i in range(2)]
        d_vlo = [sem(f"d_vlo{i}") for i in range(2)]
        d_out = sem("d_out")
        qk_filled, qk_act, qk_dve = sem("qk_filled"), sem("qk_act"), sem("qk_dve")
        block_filled, block_copied = sem("block_filled"), sem("block_copied")
        v_filled, v_act, v_dve = sem("v_filled"), sem("v_act"), sem("v_dve")
        tr_filled, tr_act, tr_dve = sem("tr_filled"), sem("tr_act"), sem("tr_dve")
        wo_filled, x_added = sem("wo_filled"), sem("x_added")
        scores_ready, pT_ready, p_hi, p_lo = sem("scores_ready"), sem("pT_ready"), sem("p_hi"), sem("p_lo")
        o_filled, o_hi, o_lo = sem("o_filled"), sem("o_hi"), sem("o_lo")
        wk_hi_done, wk_split, wv_hi_done, wv_split = (sem(n) for n in ("wk_hi_done", "wk_split", "wv_hi_done", "wv_split"))
        wq_hi_done, wq_split, wo_hi_done, wo_split = (sem(n) for n in ("wq_hi_done", "wq_split", "wo_hi_done", "wo_split"))
        pos_step, hot_done, const_set, cap_step = sem("pos_step"), sem("hot_done"), sem("const_set"), sem("cap_step")
        table_hi_done, table_split = sem("table_hi_done"), sem("table_split")
        small_turned, small_copied = sem("small_turned"), sem("small_copied")
        b_hi_done, b_split = sem("b_hi_done"), sem("b_split")
        wv0_hi_done, wv0_split = sem("wv0_hi_done"), sem("wv0_split")
        blocks_reduced, blocks_flagged, w_masked = sem("blocks_reduced"), sem("blocks_flagged"), sem("w_masked")
        ln_stats, ln_aggr, ln_var, ln_rstd, ln_out = (sem(n) for n in ("ln_stats", "ln_aggr", "ln_var", "ln_rstd", "ln_out"))
        biased = sem("biased")
        rope_sin, rotated = sem("rope_sin"), sem("rotated")
        capped, maxed, shift_done, exp_done, summed, inverted, probs_ready = (sem(n) for n in (
            "capped", "maxed", "shift_done", "exp_done", "summed", "inverted", "probs_ready"))
        f_mg, f_logit, f_max, f_cmp, f_centred, f_exp, f_rank, f_chosen, f_sum, f_inv, f_scale, f_gated, f_gT, f_gT_hi, f_gT_lo, f_y, f_out = (
            sem(n) for n in ("f_mg", "f_logit", "f_max", "f_cmp", "f_centred", "f_exp", "f_rank", "f_chosen",
                             "f_sum", "f_inv", "f_scale", "f_gated", "f_gT", "f_gT_hi", "f_gT_lo", "f_y", "f_out"))

        TR_W = TILES
        TR_SETUP = TR_W + CH
        TR_STAGE1 = TR_SETUP + 4 * PAIRS
        QK_K = UNITS
        QK_Q = QK_K + KV_HEADS * UNITS
        ADDED_1 = TILES
        LAST = KV_HEADS * UNITS - 1

        def norm1_index(p):
            return 0 if isinstance(p, int) and p == 0 else 2 * p - 1

        def norm2_index(p):
            return 2 * PAIRS - 1 if isinstance(p, int) and p == PAIRS - 1 else 2 * p + 2

        def linear_x(p, j):
            if isinstance(p, int) and p == PAIRS - 1 and j == 1:
                return extra_hi, extra_lo
            return xn1T_hi, xn1T_lo

        def v_bank(v):
            return SC[v % 2][:, :].rearrange("p (t g d) -> p t g d", t=2, g=2)

        def v_stage(v, part):
            return soft[:, 2 * (v % 2) + part, :].rearrange("p (g t d) -> p t g d", t=2, g=2)

        def o_bank(b):
            return b[:, :].rearrange("p (i h q) -> p i h q", i=2, h=GROUP)

        def o_view(m, r, par):
            v = m.rearrange("p h (r i par q) -> p r par i h q", r=2, i=2, par=2)
            return v[:, r, par]

        def use_parity(use):
            return use[1] % 2

        def row_half(par):
            return slice(par * HALF, (par + 1) * HALF)

        block = stack.enter_context(nc.Block())

        @block.sync
        def _(sp):
            def load_ctx(n):
                sp.dma_start(raw[:, n, :], ctx_rows[n * P:(n + 1) * P, :]).then_inc(d_ctx[n], 16)

            def load_x(n):
                sp.dma_start(xacc[:, n, :], x_rows[n * P:(n + 1) * P, :]).then_inc(d_x[n], 16)

            def load_pair(dst, src, p, done):
                sp.dma_start(dst, src.rearrange("(c k) n -> k c n", k=P)[:, :, bass.ds(p * PW, PW)]).then_inc(done, 16)

            def load_wq(g):
                sp.dma_start(wq_raw, wq.rearrange("(c k) n -> k c n", k=P)[:, :, bass.ds(g * HW, HW)]).then_inc(d_wq, 16)

            def load_wo(g):
                sp.dma_start(wo_raw, wo[bass.ds(g * HW, HW), :].rearrange("(h d) n -> d h n", d=P)).then_inc(d_wo, 16)

            sp.dma_start(ident, consts[:, C_IDENT:C_BLOCKS]).then_inc(d_ident, 16)
            for n in range(TILES):
                load_ctx(n)
            load_pair(wv_raw, wv, 0, d_wv)
            sp.dma_start(pos_i, pos_row.unsqueeze(0).broadcast_to([P, TOK])).then_inc(d_pos, 16)
            sp.dma_start(con[:, C_BLOCKS:C_END], consts[:, C_BLOCKS:C_END]).then_inc(d_con, 16)
            sp.dma_start(table, consts[:, C_END:C_ALL]).then_inc(d_con, 16)
            sp.dma_start(m_rows.bitcast(I32), w_mask.rearrange("(c p) k -> p c k", p=P)).then_inc(d_mask, 16)
            load_pair(wk_raw, wk, 0, d_wk)
            def store_v(p, v):
                for part, done in enumerate((d_vhi, d_vlo)):
                    sp.wait_ge((v_act, v_dve)[part], 4 * p + v + 1)
                    sp.dma_start(
                        v_dram[part, bass.ds(2 * p, 2), :, 2 * v:2 * v + 2, :].rearrange("g p t d -> p g (t d)"),
                        soft[:, 2 * (v % 2) + part, :].rearrange("p (g n) -> p g n", g=2),
                    ).then_inc(done[v % 2], 16)

            def next_wv(p):
                if isinstance(p, int) and p == 0:
                    sp.wait_ge(wv0_split, CH)
                else:
                    sp.wait_ge(wv_split, p)
                load_pair(wv_raw, wv, p + 1, d_wv)

            def next_wk(p):
                sp.wait_ge(wk_split, p + 1)
                load_pair(wk_raw, wk, p + 1, d_wk)

            store_v(0, 0)
            sp.dma_start(w_rows, w_attn.rearrange("(c p) k -> p c k", p=P)).then_inc(d_w, 16)
            load_x(0)
            load_x(1)
            store_v(0, 1)
            sp.dma_start(bias_bc, bias.unsqueeze(0).broadcast_to([P, E])).then_inc(d_bias, 16)
            load_x(2)
            load_x(3)
            next_wv(0)
            next_wk(0)
            store_v(0, 2)
            store_v(0, 3)
            for n in range(4, TILES):
                load_x(n)
            sp.wait_ge(table_split, 1)
            for h in range(2):
                sp.dma_start(cap[h * HALF:(h + 1) * HALF, :, :].bitcast(I32),
                             smask.rearrange("b q k -> q b k")).then_inc(d_cap, 16)
            store_v(1, 0)
            store_v(1, 1)

            with sp.Fori(1, PAIRS - 1) as p:
                next_wv(p)
                store_v(p, 2)
                next_wk(p)
                store_v(p, 3)
                store_v(p + 1, 0)
                store_v(p + 1, 1)
            sp.wait_ge(tr_filled, TR_SETUP + 4 * (PAIRS - 1) + 2)
            load_wq(0)
            store_v(PAIRS - 1, 2)
            store_v(PAIRS - 1, 3)
            sp.wait_ge(wo_filled, TILES)

            def load_v(g, first=False):
                if not first:
                    sp.wait_ge(o_filled, 4 * g)
                for n in range(2):
                    for par in range(2):
                        sp.dma_start(v_twice[row_half(n), :, :].rearrange("k (t par) d -> k par t d", par=2)[:, par].bitcast(F32),
                                     v_dram[0, bass.ds(g, 1), row_half(par)].rearrange("o k t d -> (o k) t d")
                                     ).then_inc(d_v, 16)
                sp.dma_start(v_low.bitcast(F32), v_dram[1, bass.ds(g, 1)].rearrange("o k t d -> (o k) t d")).then_inc(d_v, 16)

            for n in range(2):
                sp.wait_ge(d_vhi[n], 32 * PAIRS)
                sp.wait_ge(d_vlo[n], 32 * PAIRS)
            load_v(0, True)
            sp.dma_start(ar_rows[0:ER, :], lora_a.rearrange("e r k -> (e r) k")).then_inc(d_small, 16)
            sp.dma_start(ar_rows[ER:ER + EXPERTS, :], w_router).then_inc(d_small, 16)
            for c in range(CH):
                sp.dma_start(b_rows[:, c, :].rearrange("p (e r) -> p e r", e=EXPERTS),
                             lora_b[:, c * P:(c + 1) * P, :].rearrange("e p r -> p e r")).then_inc(d_small, 16)
            sp.wait_ge(tr_filled, TR_STAGE1)
            load_wo(0)

            def stage2(g):
                sp.wait_ge(wq_split, CH * (g + 1))
                load_wq(g + 1)
                sp.wait_ge(wo_split, GROUP * (g + 1))
                load_wo(g + 1)
                load_v(g + 1)

            with sp.Fori(0, KV_HEADS - 1) as g:
                stage2(g)

            for n in range(TILES):
                sp.wait_ge(f_out, n + 1)
                sp.dma_start(out_rows[n * P:(n + 1) * P, :], xacc[:, n, :]).then_inc(d_out, 16)
            sp.wait_ge(d_out, 16 * TILES)

        @block.tensor
        def _(pe):
            def mm3(dst, lhs, rhs, first, last):
                pe.matmul(dst, lhs[0], rhs[0], start=first, stop=False)
                pe.matmul(dst, lhs[0], rhs[1], start=False, stop=False)
                return pe.matmul(dst, lhs[1], rhs[0], start=False, stop=last)

            def transpose_tile(dst, rows, n=CH):
                for c in range(n):
                    t = pe.transpose(dst[:, c * P:(c + 1) * P], rows[:, c * P:(c + 1) * P], ident)
                return t

            def project_v(p, v, tiles=(0, 1), first=False):
                if 0 in tiles and (not isinstance(p, int) or 4 * p + v >= 2):
                    pe.wait_ge(v_dve, 4 * p + v - 1)
                for j in tiles:
                    tile = 2 * v + j
                    tok = slice(tile * P, (tile + 1) * P)
                    for c in range(CH):
                        if first and j == 0:
                            pe.wait_ge(wv0_split, c + 1)
                        m = mm3(SC[v % 2][:, j * PW:(j + 1) * PW], (ctxT_hi[:, c, tok], ctxT_lo[:, c, tok]),
                                (wv_hi[:, c, :], wv_lo[:, c, :]), c == 0, c == CH - 1)
                if 1 in tiles:
                    m.then_inc(v_filled, 1)

            pe.wait_ge(d_ident, 16)
            def transpose_ctx(n):
                pe.wait_ge(d_ctx[n], 16)
                if n >= 6:
                    pe.wait_ge(tr_dve, n - 5)
                transpose_tile(CTX_T[n], raw[:, n, :]).then_inc(tr_filled, 1)

            def rope_table(t):
                pe.wait_ge(hot_done, (t + 1) * (MAX_POS // P))
                for c in range(MAX_POS // P):
                    for part in (table_hi, table_lo):
                        m = pe.matmul(QK[t][:, :], part[:, c * P:(c + 1) * P], onehot[t][:, c, :],
                                      start=(c == 0 and part is table_hi), stop=(c == MAX_POS // P - 1 and part is table_lo))
                m.then_inc(qk_filled, 1)

            for n in range(TILES):
                transpose_ctx(n)
            pe.wait_ge(tr_dve, TILES)
            project_v(0, 0, first=True)
            project_v(0, 1)
            project_v(0, 2)
            pe.wait_ge(table_split, 1)
            rope_table(0)
            rope_table(1)
            pe.wait_ge(blocks_reduced, 1)
            pe.matmul(WO[0][:, 0:CH * (E // SPARSE_BLOCK)], con[:, C_BLOCKS:C_IOTA],
                      block_sum[:, :, :].rearrange("p c b -> p (c b)"), start=True, stop=True).then_inc(block_filled, 1)

            def transpose_w(c):
                pe.wait_ge(w_masked, 1)
                for r in range(CH):
                    m = pe.transpose(W_T[c][:, r * P:(r + 1) * P], w_rows[:, r, c * P:(c + 1) * P], ident)
                m.then_inc(tr_filled, 1)

            def transpose_small():
                pe.wait_ge(d_small, 16 * (2 + CH))
                pe.wait_ge(qk_dve, QK_Q + GROUP - 1)
                for c in range(CH):
                    m = pe.transpose(SMALL_T[0][:, c * P:c * P + ER + EXPERTS], ar_rows[:, c * P:(c + 1) * P],
                                     con[0:ER + EXPERTS, 0:ER + EXPERTS])
                m.then_inc(small_turned, 1)
                for c in range(CH):
                    m = pe.transpose(SMALL_T[1][0:ER, c * P:(c + 1) * P], b_rows[:, c, :], ident)
                m.then_inc(small_turned, 1)

            def project_k_tile(p, h, t):
                pe.wait_ge(qk_dve, QK_K + 4 * p + 2 * h + t - 1)
                tok = slice(t * UTOK, (t + 1) * UTOK)
                col = slice(h * HEAD_DIM, (h + 1) * HEAD_DIM)
                for c in range(CH):
                    m = mm3(QK[t][:, :], (wk_hi[:, c, col], wk_lo[:, c, col]),
                            (ctxT_hi[:, c, tok], ctxT_lo[:, c, tok]), c == 0, c == CH - 1)
                m.then_inc(qk_filled, 1)

            def project_k(p, h):
                for t in range(UNITS):
                    project_k_tile(p, h, t)

            def project_k0(n):
                project_k_tile(0, n // 2, n % 2)

            def transpose_norm(p, second):
                for j in range(2):
                    k = 4 * p + 2 * second + j
                    pe.wait_ge(ln_out, 2 * (norm2_index(p) if second else norm1_index(p)) + j + 1)
                    pe.wait_ge(tr_dve, TR_W + j + 1 if isinstance(k, int) and k < 2 else TR_SETUP + k - 1)
                    transpose_tile(TR[j], (norm2 if second else norm1)[:, j, :]).then_inc(tr_filled, 1)

            def linear(p, j):
                pe.wait_ge(tr_dve, TR_SETUP + 4 * p + j + 1)
                hi, lo = linear_x(p, j)
                for c in range(CH):
                    cols = slice(c * P, (c + 1) * P)
                    m = mm3(WO[j][:, :], (hi[:, cols], lo[:, cols]),
                            (wT_hi[:, c, :], wT_lo[:, c, :]), c == 0, c == CH - 1)
                m.then_inc(wo_filled, 1)

            project_v(0, 3)
            pe.wait_ge(wk_split, 1)
            project_k0(0)
            project_k0(1)
            transpose_w(0)
            transpose_w(1)
            project_k0(2)
            transpose_w(2)
            transpose_w(3)
            transpose_norm(0, 0)
            pe.wait_ge(wv_split, 1)
            project_v(1, 0)
            linear(0, 0)
            project_v(1, 1, tiles=(0,))
            linear(0, 1)
            project_k0(3)
            project_v(1, 1, tiles=(1,))
            transpose_norm(0, 1)
            with pe.Fori(1, PAIRS - 1) as p:
                transpose_norm(p, 0)
                project_v(p, 2)
                linear(p, 0)
                project_v(p, 3)
                linear(p, 1)
                pe.wait_ge(wk_split, p + 1)
                project_k(p, 0)
                transpose_norm(p, 1)
                project_k(p, 1)
                pe.wait_ge(wv_split, p + 1)
                project_v(p + 1, 0)
                project_v(p + 1, 1)
            transpose_norm(PAIRS - 1, 0)
            project_v(PAIRS - 1, 2)
            project_v(PAIRS - 1, 3)
            pe.wait_ge(wk_split, PAIRS)
            project_k(PAIRS - 1, 0)
            project_k(PAIRS - 1, 1)
            linear(PAIRS - 1, 0)
            linear(PAIRS - 1, 1)

            def project_q(t, h, chunks=range(CH), new_wq=None):
                tok = slice(t * UTOK, (t + 1) * UTOK)
                col = slice(h * HEAD_DIM, (h + 1) * HEAD_DIM)
                for c in chunks:
                    if new_wq is not None and h == 0:
                        pe.wait_ge(wq_split, new_wq + c + 1)
                    m = mm3(RING[h][:, :], (wq_hi[:, c, col], wq_lo[:, c, col]),
                            (xnT_hi[:, c, tok], xnT_lo[:, c, tok]), c == 0, c == CH - 1)
                if c == CH - 1:
                    m.then_inc(qk_filled, 1)

            def next_q(g, t, h, chunks=range(CH)):
                if chunks[0] == 0:
                    pe.wait_ge(x_added, ADDED_1 + UTILES * (2 * g + t) + h - 3)
                if t == 0 and h == 0 and chunks[0] == 0:
                    pe.wait_ge(tr_dve, TR_SETUP + 4 * PAIRS)
                if t == 0 and h == 1 and chunks[0] == 0:
                    pe.wait_ge(small_copied, 2)
                project_q(1 - t, h, chunks, CH * (g + 1) if t else None)

            def scores(g, u, t, pairs=(0, 1)):
                for hp in pairs:
                    pe.wait_ge(rotated, QK_Q + GROUP * u + 2 * hp + 2)
                    for b in range(UB):
                        m = pe.matmul(SC[hp][:, b * S:(b + 1) * S], q_rot[:, hp, b, :, :].rearrange("p h q -> p (h q)"),
                                      k_rot[:, bass.ds(g, 1), t * UTOK + b * S:t * UTOK + (b + 1) * S]
                                      .rearrange("p o k -> p (o k)"), start=True, stop=True)
                    m.then_inc(scores_ready, 1)

            def transpose_probs(u, hp):
                pe.wait_ge(probs_ready, 2 * u + hp + 1)
                transpose_tile(SC[hp], probs[:, hp, :]).then_inc(pT_ready, 1)

            def times_v(g, u, t):
                pe.wait_ge(d_v, 16 * 5 * g + 16 * 5)
                pe.wait_ge(p_lo, 4 * u + 4)
                for r in range(2):
                    banks = (TR, SC)[r]
                    for full in (True, False):
                        for i in range(2):
                            for par in range(2):
                                bp = 2 * r + i
                                cols = slice(bp * P, (bp + 1) * P)
                                dst = banks[par][:, i * 256:(i + 1) * 256]
                                tile = t * UTILES + bp
                                if full:
                                    m = pe.matmul(dst, v_twice[:, 2 * tile + par, :], pT[:, par, :, cols],
                                                  start=(i == 0), stop=False, skip_group_check=True)
                                else:
                                    m = pe.matmul(dst, v_low[row_half(par), tile, :], pT[row_half(par), par, :, cols],
                                                  start=False, stop=(i == 1), skip_group_check=True)
                    m.then_inc(o_filled, 1)

            def project_out(u, i, dst):
                pe.wait_ge(o_lo, 4 * u + 2 * (i // 2) + 2)
                tok = slice(i * P, (i + 1) * P)
                for h in range(GROUP):
                    m = mm3(dst[:, :], (oT_hi[:, h, tok], oT_lo[:, h, tok]),
                            (wo_hi[:, h, :], wo_lo[:, h, :]), h == 0, h == GROUP - 1)
                m.then_inc(wo_filled, 1)

            def attend(g, t):
                u = 2 * g + t
                scores(g, u, t)
                next_q(g, t, 0)
                next_q(g, t, 1)
                transpose_probs(u, 0)
                next_q(g, t, 2, range(0, 1))
                transpose_probs(u, 1)
                next_q(g, t, 2, range(1, CH))
                next_q(g, t, 3, range(0, CH // 2))
                times_v(g, u, t)
                next_q(g, t, 3, range(CH // 2, CH))

            def output_tile(g, u, i):
                pe.wait_ge(wo_split, GROUP * (g + 1))
                pe.wait_ge(qk_dve, QK_Q + GROUP * (u + 1) + i + 1)
                project_out(u, i, RING[i])

            def unit(g, t):
                attend(g, t)
                for i in range(UTILES):
                    output_tile(g, 2 * g + t, i)

            for h in range(GROUP):
                if h < 2:
                    pe.wait_ge(qk_dve, QK_Q - 1 + h)
                else:
                    pe.wait_ge(x_added, ADDED_1 - 3 + h)
                project_q(0, h, new_wq=0)
            transpose_norm(PAIRS - 1, 1)
            transpose_small()
            with pe.Fori(0, KV_HEADS - 1) as g:
                unit(g, 0)
                unit(g, 1)
            attend(KV_HEADS - 1, 0)

            def ffn_transpose(*tiles):
                for n in tiles:
                    pe.wait_ge(ln_out, 4 * PAIRS + n + 1)
                    if n >= 2:
                        pe.wait_ge(tr_act, TR_STAGE1 + n - 1)
                    transpose_tile(FFN_X[n % 2], ffn_norm[:, n % UTILES, :]).then_inc(tr_filled, 1)

            def ffn_down(*tiles):
                for n in tiles:
                    if n == 0:
                        pe.wait_ge(x_added, ADDED_1 + UTILES * LAST - 1)
                    if n == UTILES:
                        pe.wait_ge(x_added, ADDED_1 + UTILES * LAST + 3)
                    pe.wait_ge(tr_act, TR_STAGE1 + n + 1)
                    j = n % UTILES
                    for c in range(CH):
                        m = pe.matmul(FFN_MG[n // UTILES][:, j * P:j * P + ER + EXPERTS],
                                      ffn_xT[:, j, c * P:(c + 1) * P], arT[:, c, :], start=(c == 0), stop=(c == CH - 1))
                    m.then_inc(f_mg, 1)

            def ffn_turn(t):
                pe.wait_ge(f_gated, t + 1)
                pe.wait_ge(x_added, ADDED_1 + UTILES * (LAST + t))
                for j in range(UTILES):
                    m = pe.transpose(FFN_GT[t][0:ER, j * P:(j + 1) * P], gated[:, j, :], ident)
                m.then_inc(f_gT, 1)

            def ffn_up(*tiles):
                for n in tiles:
                    pe.wait_ge(b_split, 1)
                    pe.wait_ge(f_gT_lo, n // 2 + 1)
                    if n < 2:
                        pe.wait_ge(x_added, ADDED_1 + UTILES * LAST + n + 1)
                    if n == UTILES:
                        pe.wait_ge(f_out, 1)
                    j = n % UTILES
                    cols = slice(j * P, (j + 1) * P)
                    pe.matmul(FFN_Y[n][:, :], gm_split[:, cols], b_twice, start=True, stop=False)
                    pe.matmul(FFN_Y[n][:, :], gm_split[0:ER, cols], b_low, start=False, stop=True).then_inc(f_y, 1)

            def last_out(i):
                project_out(LAST, i, LAST_OUT[i])

            output_tile(KV_HEADS - 1, LAST - 1, 0)
            pe.wait_ge(o_lo, 4 * (LAST - 1) + 4)
            scores(KV_HEADS - 1, LAST, 1, pairs=(0,))
            output_tile(KV_HEADS - 1, LAST - 1, 1)
            scores(KV_HEADS - 1, LAST, 1, pairs=(1,))
            output_tile(KV_HEADS - 1, LAST - 1, 2)
            output_tile(KV_HEADS - 1, LAST - 1, 3)
            transpose_probs(LAST, 0)
            transpose_probs(LAST, 1)
            times_v(KV_HEADS - 1, LAST, 1)
            ffn_transpose(0, 1)
            last_out(0)
            last_out(1)
            ffn_transpose(2, 3)
            last_out(2)
            last_out(3)
            ffn_down(0, 1, 2, 3)
            ffn_transpose(4, 5)
            ffn_down(4, 5)
            ffn_transpose(6, 7)
            ffn_turn(0)
            ffn_down(6, 7)
            ffn_up(0, 1, 2, 3)
            ffn_turn(1)
            ffn_up(4, 5, 6, 7)

        @block.scalar
        def _(act):
            def copy(dst, src):
                return act.activation(dst, src, ACT.Copy)

            def tok_tile(m, n):
                return m[:, :, bass.ds(n * P, P)]

            def bank_chunks(b):
                return b[:, :].rearrange("p (c t) -> p c t", c=CH)

            def swap_halves(use, src):
                b = use_parity(use)
                act.wait_ge(qk_filled, use[0] + use[1] + 1)
                act.wait_ge(rotated, use[0] + use[1] - 1)
                copy(swapped[0:HALF, b, :], src[HALF:P, :])
                copy(swapped[HALF:P, b, :], src[0:HALF, :]).then_inc(qk_act, 1)

            def v_hi_part(p, v):
                act.wait_ge(v_filled, 4 * p + v + 1)
                if not isinstance(p, int) or 2 * p + v // 2 > 0:
                    act.wait_ge(d_vhi[v % 2], 16 * (2 * p + v // 2))
                copy(v_stage(v, 0).bitcast(F32R), v_bank(v)).then_inc(v_act, 1)

            def ctx_hi(n):
                act.wait_ge(tr_filled, n + 1)
                copy(tok_tile(ctxT_hi, n), bank_chunks(CTX_T[n])).then_inc(tr_act, 1)

            def cosines(t):
                act.wait_ge(qk_filled, t + 1)
                tok = slice(t * UTOK, (t + 1) * UTOK)
                copy(cosT[0:HALF, tok], QK[t][0:HALF, :])
                copy(cosT[HALF:P, tok], QK[t][0:HALF, :]).then_inc(qk_act, 1)

            for n in range(TILES):
                ctx_hi(n)
            act.wait_ge(d_wv, 16)
            for c in range(CH):
                copy(wv_hi[:, c, :], wv_raw[:, c, :]).then_inc(wv0_hi_done, 1)
            v_hi_part(0, 0)
            act.wait_ge(d_con, 32)
            copy(table_hi, table).then_inc(table_hi_done, 1)
            v_hi_part(0, 1)
            act.wait_ge(d_wk, 16)
            copy(wk_hi, wk_raw).then_inc(wk_hi_done, 1)
            v_hi_part(0, 2)
            cosines(0)
            cosines(1)
            act.wait_ge(block_filled, 1)
            copy(block_on[:, :, :].rearrange("p c b -> p (c b)"), WO[0][:, 0:CH * (E // SPARSE_BLOCK)]).then_inc(block_copied, 1)
            v_hi_part(0, 3)

            def weight_hi(c):
                act.wait_ge(tr_filled, TR_W + c + 1)
                copy(wT_hi[:, c, :], W_T[c][:, :]).then_inc(tr_act, 1)

            def small_weights():
                act.wait_ge(small_turned, 1)
                copy(arT[:, :, :], bank_chunks(SMALL_T[0])[:, :, 0:ER + EXPERTS]).then_inc(small_copied, 1)
                act.wait_ge(small_turned, 2)
                copy(bT[:, :], SMALL_T[1][0:ER, :]).then_inc(small_copied, 1)

            def first_norm_hi(p, j):
                act.wait_ge(tr_filled, TR_SETUP + 4 * p + j + 1)
                hi = linear_x(p, j)[0]
                if j and hi is xn1T_hi:
                    act.wait_ge(wo_filled, 2 * p + 1)
                copy(hi, TR[j][:, :]).then_inc(tr_act, 1)

            def round_wk(p):
                act.wait_ge(d_wk, 16 * p + 16)
                act.wait_ge(qk_filled, QK_K + 4 * p)
                copy(wk_hi, wk_raw).then_inc(wk_hi_done, 1)

            def second_norm_hi(p):
                for j in range(2):
                    act.wait_ge(tr_filled, TR_SETUP + 4 * p + 2 + j + 1)
                    copy(tok_tile(xnT_hi, 2 * p + j), bank_chunks(TR[j])).then_inc(tr_act, 1)

            def swap_k(p, h):
                for t in range(UNITS):
                    swap_halves((QK_K + 4 * p, 2 * h + t), QK[t])

            def round_wv(p):
                act.wait_ge(d_wv, 16 * p + 16)
                copy(wv_hi, wv_raw).then_inc(wv_hi_done, 1)

            round_wv(1)
            swap_halves((QK_K, 0), QK[0])
            swap_halves((QK_K, 1), QK[1])
            weight_hi(0)
            weight_hi(1)
            swap_halves((QK_K, 2), QK[0])
            weight_hi(2)
            weight_hi(3)
            first_norm_hi(0, 0)
            v_hi_part(1, 0)
            first_norm_hi(0, 1)
            swap_halves((QK_K, 3), QK[1])
            second_norm_hi(0)
            v_hi_part(1, 1)
            with act.Fori(1, PAIRS - 1) as p:
                first_norm_hi(p, 0)
                round_wk(p)
                v_hi_part(p, 2)
                first_norm_hi(p, 1)
                v_hi_part(p, 3)
                round_wv(p + 1)
                swap_k(p, 0)
                second_norm_hi(p)
                swap_k(p, 1)
                v_hi_part(p + 1, 0)
                v_hi_part(p + 1, 1)
            first_norm_hi(PAIRS - 1, 0)
            round_wk(PAIRS - 1)
            v_hi_part(PAIRS - 1, 2)
            v_hi_part(PAIRS - 1, 3)
            first_norm_hi(PAIRS - 1, 1)
            swap_k(PAIRS - 1, 0)
            swap_k(PAIRS - 1, 1)

            def round_wq(g):
                act.wait_ge(d_wq, 16 * g + 16)
                act.wait_ge(qk_filled, QK_Q + 2 * GROUP * g)
                for c in range(CH):
                    copy(wq_hi[:, c, :], wq_raw[:, c, :]).then_inc(wq_hi_done, 1)

            def round_wo(g):
                act.wait_ge(d_wo, 16 * g + 16)
                act.wait_ge(wo_filled, TILES * (g + 1))
                for h in range(GROUP):
                    copy(wo_hi[:, h, :], wo_raw[:, h, :]).then_inc(wo_hi_done, 1)

            def swap_q(u, h):
                swap_halves((QK_Q + GROUP * u, h), RING[h])

            def exponentials(u):
                for hp in range(2):
                    act.wait_ge(shift_done, 2 * u + hp + 1)
                    act.activation(shifted[:, hp, :], shifted[:, hp, :], ACT.Exp, scale=SCORE_SCALE).then_inc(exp_done, 1)

            def probs_hi(u, hp):
                act.wait_ge(pT_ready, 2 * u + hp + 1)
                for par in range(2):
                    copy(pT[row_half(par), par, hp, :], SC[hp][row_half(par), :]).then_inc(p_hi, 1)

            def output_hi(u, r):
                act.wait_ge(o_filled, 2 * u + r + 1)
                for par in range(2):
                    copy(o_view(oT_hi, r, par), o_bank((TR, SC)[r][par])).then_inc(o_hi, 1)

            def unit(g, t, more=True):
                u = 2 * g + t
                if t == 0:
                    round_wo(g)
                exponentials(u)
                swap_q(u + 1, 0)
                probs_hi(u, 0)
                probs_hi(u, 1)
                swap_q(u + 1, 1)
                output_hi(u, 0)
                output_hi(u, 1)
                swap_q(u + 1, 2)
                swap_q(u + 1, 3)
                if t == 0 and more:
                    round_wq(g + 1)

            round_wq(0)
            for h in range(GROUP):
                swap_q(0, h)
            second_norm_hi(PAIRS - 1)
            small_weights()
            with act.Fori(0, KV_HEADS - 1) as g:
                unit(g, 0)
                unit(g, 1)
            unit(KV_HEADS - 1, 0, more=False)

            def ffn_copy_xT(*tiles):
                for n in tiles:
                    act.wait_ge(tr_filled, TR_STAGE1 + n + 1)
                    if n >= UTILES:
                        act.wait_ge(f_mg, n - UTILES + 1)
                    copy(ffn_xT[:, n % UTILES, :], FFN_X[n % 2][:, :]).then_inc(tr_act, 1)

            def ffn_exp(t):
                act.wait_ge(f_centred, t + 1)
                act.activation(g_exp[:, :, :], g_exp[:, :, :], ACT.Exp).then_inc(f_exp, 1)

            def ffn_gT_hi(t):
                act.wait_ge(f_gT, t + 1)
                if t:
                    act.wait_ge(f_y, UTILES)
                copy(gm_split[0:ER, :], FFN_GT[t][0:ER, :]).then_inc(f_gT_hi, 1)

            act.wait_ge(qk_filled, QK_Q + GROUP * (LAST + 1))
            copy(b_twice[0:ER, :], bT[:, :])
            copy(b_twice[ER:P, :], bT[:, :]).then_inc(b_hi_done, 1)
            exponentials(LAST)
            probs_hi(LAST, 0)
            probs_hi(LAST, 1)
            output_hi(LAST, 0)
            output_hi(LAST, 1)
            ffn_copy_xT(0, 1, 2, 3, 4, 5)
            ffn_exp(0)
            ffn_copy_xT(6, 7)
            ffn_gT_hi(0)
            ffn_exp(1)
            ffn_gT_hi(1)

        @block.vector
        def _(dve):
            def tt(dst, a, b, op):
                return dve.tensor_tensor(dst, a, b, op)

            def tok_tile(m, n):
                return m[:, :, bass.ds(n * P, P)]

            def bank_chunks(b):
                return b[:, :].rearrange("p (c t) -> p c t", c=CH)

            def by_batch(a):
                return a.rearrange("p (b k) -> p b k", k=S)

            def lo_part(dst_lo, value, hi):
                return tt(dst_lo, value, hi.bitcast(F32), ALU.subtract)

            def carry_wait():
                dve.memset(tick[:, :], 0.0)

            def layernorm_stats(n, m, rows):
                carry_wait()
                for j in range(m):
                    dve.bn_stats(stats[:, j, :], rows(j)).then_inc(ln_stats, 1)
                dve.wait_ge(ln_stats, n + m)
                carry_wait()
                for j in range(m):
                    dve.bn_aggr(mean_var[:, j, :], stats[:, j, :]).then_inc(ln_aggr, 1)
                for j in range(m):
                    dve.wait_ge(ln_aggr, n + j + 1)
                    dve.tensor_scalar(var_eps[:, j, :], mean_var[:, j, 1:2], EPS, None, ALU.add).then_inc(ln_var, 1)

            def layernorm_apply(n, m, rows, dst):
                for j in range(m):
                    dve.wait_ge(ln_rstd, n + j + 1)
                    dve.tensor_scalar(dst(j), rows(j), mean_var[:, j, 0:1], rstd[:, j, :],
                                      ALU.subtract, ALU.mult).then_inc(ln_out, 1)

            def layernorm_pair(pair, rows, dst):
                layernorm_stats(2 * pair, 2, rows)
                layernorm_apply(2 * pair, 2, rows, dst)

            def x_rows_of(p):
                return lambda j: xacc[:, bass.ds(2 * p + j, 1), :].rearrange("p o e -> p (o e)")

            def norm1_of(j):
                return norm1[:, j, :]

            def norm2_of(j):
                return norm2[:, j, :]

            def first_norm(p):
                layernorm_pair(norm1_index(p), x_rows_of(p), norm1_of)

            def v_lo_part(p, v):
                dve.wait_ge(v_act, 4 * p + v + 1)
                if not isinstance(p, int) or 2 * p + v // 2 > 0:
                    dve.wait_ge(d_vlo[v % 2], 16 * (2 * p + v // 2))
                tt(v_stage(v, 1).bitcast(F32R), v_bank(v), v_stage(v, 0), ALU.subtract).then_inc(v_dve, 1)

            def ctx_lo(n):
                dve.wait_ge(tr_act, n + 1)
                lo_part(tok_tile(ctxT_lo, n), bank_chunks(CTX_T[n]), tok_tile(ctxT_hi, n)).then_inc(tr_dve, 1)

            dve.memset(minus_half[:, :], -0.5).then_inc(const_set, 1)
            for n in range(TILES):
                ctx_lo(n)
            for c in range(CH):
                dve.wait_ge(wv0_hi_done, c + 1)
                lo_part(wv_lo[:, c, :], wv_raw[:, c, :], wv_hi[:, c, :]).then_inc(wv0_split, 1)
            dve.wait_ge(d_pos, 16)
            dve.tensor_scalar(pos_f, pos_i, 0.0, float(MAX_POS), ALU.is_lt, ALU.mult).then_inc(pos_step, 1)
            dve.wait_ge(pos_step, 1)
            tt(pos_f, pos_f, pos_i, ALU.add).then_inc(pos_step, 1)
            v_lo_part(0, 0)
            dve.wait_ge(d_con, 32)
            dve.wait_ge(pos_step, 2)
            for t in range(UNITS):
                for c in range(MAX_POS // P):
                    limit, op = {0: (0.0, ALU.max), MAX_POS // P - 1: (float(MAX_POS - 1), ALU.min)}.get(c, (None, None))
                    number = con[:, C_IOTA + c:C_IOTA + c + 1]
                    dst, src = onehot[t][:, c, :], pos_f[:, t * UTOK:(t + 1) * UTOK]
                    if limit is None:
                        dve.tensor_scalar(dst, src, number, None, ALU.is_equal).then_inc(hot_done, 1)
                    else:
                        dve.tensor_scalar(dst, src, limit, number, op, ALU.is_equal).then_inc(hot_done, 1)
            dve.wait_ge(table_hi_done, 1)
            lo_part(table_lo, table, table_hi).then_inc(table_split, 1)
            v_lo_part(0, 1)
            dve.wait_ge(d_mask, 16)
            dve.tensor_reduce(block_sum[:, :, :], m_rows.bitcast(I32).rearrange("p c (b k) -> p c b k", k=SPARSE_BLOCK),
                              AX.X, ALU.add).then_inc(blocks_reduced, 1)
            v_lo_part(0, 2)

            def sines(t):
                dve.wait_ge(qk_act, t + 1)
                tok = slice(t * UTOK, (t + 1) * UTOK)
                dve.tensor_scalar(sinT[0:HALF, tok], QK[t][HALF:P, :], -1.0, None, ALU.mult).then_inc(rotated, 1)
                dve.tensor_copy(sinT[HALF:P, tok], QK[t][HALF:P, :]).then_inc(qk_dve, 1)

            sines(0)
            sines(1)
            dve.wait_ge(block_copied, 1)
            dve.tensor_scalar(block_sum[:, :, :], block_on[:, :, :], 0.0, None, ALU.is_gt).then_inc(blocks_flagged, 1)
            dve.wait_ge(d_x[0], 16)
            dve.wait_ge(d_x[1], 16)
            layernorm_stats(2 * norm1_index(0), 2, x_rows_of(0))
            v_lo_part(0, 3)
            layernorm_apply(2 * norm1_index(0), 2, x_rows_of(0), norm1_of)

            def weight_lo(c):
                dve.wait_ge(tr_act, TR_W + c + 1)
                lo_part(wT_lo[:, c, :], W_T[c][:, :], wT_hi[:, c, :]).then_inc(tr_dve, 1)

            def rope(use, src, dst, t):
                b = use_parity(use)
                n = use[0] + use[1] - QK_K
                tok = slice(t * UTOK, (t + 1) * UTOK)
                dve.wait_ge(rotated, use[0] + use[1] - 1)
                dve.wait_ge(qk_act, use[0] + use[1] + 1)
                tt(cos_part[:, b, :], src[:, :], cosT[:, tok], ALU.mult).then_inc(qk_dve, 1)
                tt(swapped[:, b, :], swapped[:, b, :], sinT[:, tok], ALU.mult).then_inc(rope_sin, 1)
                dve.wait_ge(rope_sin, n + 1)
                tt(dst, by_batch(cos_part[:, b, :]), by_batch(swapped[:, b, :]), ALU.add).then_inc(rotated, 1)

            def rope_k(p, h, t):
                dst = k_rot[:, bass.ds(2 * p + h, 1), t * UTOK:(t + 1) * UTOK].rearrange("p o k -> p (o k)")
                rope((QK_K + 4 * p, 2 * h + t), QK[t], by_batch(dst), t)

            def first_norm_lo(p, j):
                dve.wait_ge(tr_act, TR_SETUP + 4 * p + j + 1)
                hi, lo = linear_x(p, j)
                lo_part(lo, TR[j][:, :], hi).then_inc(tr_dve, 1)

            def second_norm_lo(p):
                for j in range(2):
                    dve.wait_ge(tr_act, TR_SETUP + 4 * p + 2 + j + 1)
                    lo_part(tok_tile(xnT_lo, 2 * p + j), bank_chunks(TR[j]), tok_tile(xnT_hi, 2 * p + j)).then_inc(tr_dve, 1)

            def add_linear(p, j):
                rows = x_rows_of(p)(j)
                dve.wait_ge(biased, 2 * p + j + 1)
                dve.wait_ge(wo_filled, 2 * p + j + 1)
                tt(rows, rows, WO[j][:, :], ALU.add).then_inc(x_added, 1)

            def second_norm(p):
                dve.wait_ge(x_added, 2 * p + 2)
                layernorm_pair(norm2_index(p), x_rows_of(p), norm2_of)

            rope_k(0, 0, 0)
            weight_lo(0)
            weight_lo(1)
            rope_k(0, 0, 1)
            weight_lo(2)
            weight_lo(3)
            first_norm_lo(0, 0)
            rope_k(0, 1, 0)
            v_lo_part(1, 0)
            dve.wait_ge(d_x[2], 16)
            dve.wait_ge(d_x[3], 16)
            layernorm_stats(2 * norm1_index(1), 2, x_rows_of(1))
            first_norm_lo(0, 1)
            dve.wait_ge(tr_filled, TR_SETUP + 2)
            layernorm_apply(2 * norm1_index(1), 2, x_rows_of(1), norm1_of)
            add_linear(0, 0)
            add_linear(0, 1)
            second_norm(0)
            second_norm_lo(0)
            rope_k(0, 1, 1)
            v_lo_part(1, 1)
            for n in range(4, TILES):
                dve.wait_ge(d_x[n], 16)
            with dve.Fori(1, PAIRS - 1) as p:
                first_norm_lo(p, 0)
                dve.wait_ge(tr_filled, TR_SETUP + 4 * p + 2)
                first_norm(p + 1)
                v_lo_part(p, 2)
                first_norm_lo(p, 1)
                add_linear(p, 0)
                v_lo_part(p, 3)
                add_linear(p, 1)
                second_norm(p)
                rope_k(p, 0, 0)
                rope_k(p, 0, 1)
                second_norm_lo(p)
                rope_k(p, 1, 0)
                rope_k(p, 1, 1)
                v_lo_part(p + 1, 0)
                v_lo_part(p + 1, 1)
            first_norm_lo(PAIRS - 1, 0)
            v_lo_part(PAIRS - 1, 2)
            dve.wait_ge(d_cap, 32)
            dve.tensor_scalar(cap[:, :, :], cap[:, :, :].bitcast(I32), 0.0, NO_CAP, ALU.not_equal, ALU.mult).then_inc(cap_step, 1)
            v_lo_part(PAIRS - 1, 3)
            first_norm_lo(PAIRS - 1, 1)
            dve.wait_ge(cap_step, 1)
            dve.tensor_scalar(cap[:, :, :], cap[:, :, :], MASK_FILL, None, ALU.add).then_inc(cap_step, 1)
            for h in range(2):
                for t in range(UNITS):
                    rope_k(PAIRS - 1, h, t)
            add_linear(PAIRS - 1, 0)
            add_linear(PAIRS - 1, 1)
            second_norm(PAIRS - 1)

            def spread(a):
                return a.unsqueeze(2).broadcast_to([P, UB, S])

            def cap_scores(u, t, hp):
                dve.wait_ge(scores_ready, 2 * u + hp + 1)
                tt(by_batch(shifted[:, hp, :]), by_batch(SC[hp][:, :]), cap[:, t * UB:(t + 1) * UB, :],
                   ALU.min).then_inc(capped, 1)

            def find_max(u, hp):
                dve.wait_ge(capped, 2 * u + hp + 1)
                dve.tensor_reduce(row_max[:, hp, :], by_batch(shifted[:, hp, :]), AX.X, ALU.max).then_inc(maxed, 1)

            def shift(u, hp):
                dve.wait_ge(maxed, 2 * u + hp + 1)
                tt(by_batch(shifted[:, hp, :]), by_batch(shifted[:, hp, :]), spread(row_max[:, hp, :]),
                   ALU.subtract).then_inc(shift_done, 1)

            def shifted_scores(u, t):
                cap_scores(u, t, 0)
                find_max(u, 0)
                cap_scores(u, t, 1)
                shift(u, 0)
                find_max(u, 1)
                shift(u, 1)

            def normalise(u, hp):
                dve.wait_ge(exp_done, 2 * u + hp + 1)
                dve.tensor_reduce(row_sum[:, hp, :], by_batch(shifted[:, hp, :]), AX.X, ALU.add).then_inc(summed, 1)
                dve.wait_ge(summed, 2 * u + hp + 1)
                dve.reciprocal(row_inv[:, hp, :], row_sum[:, hp, :]).then_inc(inverted, 1)
                dve.wait_ge(inverted, 2 * u + hp + 1)
                tt(by_batch(probs[:, hp, :]), by_batch(shifted[:, hp, :]), spread(row_inv[:, hp, :]),
                   ALU.mult).then_inc(probs_ready, 1)

            def probs_lo(u, hp):
                for par in range(2):
                    dve.wait_ge(p_hi, 4 * u + 2 * hp + par + 1)
                    lo_part(pT[row_half(1 - par), par, hp, :], SC[hp][row_half(par), :],
                            pT[row_half(par), par, hp, :]).then_inc(p_lo, 1)

            def output_lo(u, r):
                for par in range(2):
                    dve.wait_ge(o_hi, 4 * u + 2 * r + par + 1)
                    lo_part(o_view(oT_lo, r, par), o_bank((TR, SC)[r][par]), o_view(oT_hi, r, par)).then_inc(o_lo, 1)

            def rope_q(u, t, h):
                rope((QK_Q + GROUP * u, h), RING[h], q_rot[:, h // 2, :, h % 2, :], t)

            def add_output(u, t, i, src):
                dve.wait_ge(wo_filled, TILES + UTILES * u + i + 1)
                rows = xacc[:, t * UTILES + i, :]
                tt(rows, rows, src[:, :], ALU.add).then_inc(x_added, 1)

            def attend(g, t):
                u = 2 * g + t
                shifted_scores(u, t)
                normalise(u, 0)
                normalise(u, 1)
                probs_lo(u, 0)
                probs_lo(u, 1)
                rope_q(u + 1, 1 - t, 0)
                output_lo(u, 0)
                output_lo(u, 1)
                rope_q(u + 1, 1 - t, 1)
                rope_q(u + 1, 1 - t, 2)
                rope_q(u + 1, 1 - t, 3)

            def unit(g, t):
                attend(g, t)
                for i in range(UTILES):
                    add_output(2 * g + t, t, i, RING[i])

            for n in range(2):
                dve.wait_ge(d_vhi[n], 32 * PAIRS)
                dve.wait_ge(d_vlo[n], 32 * PAIRS)
            dve.wait_ge(cap_step, 2)
            for h in range(GROUP):
                rope_q(0, 0, h)
            second_norm_lo(PAIRS - 1)
            with dve.Fori(0, KV_HEADS - 1) as g:
                unit(g, 0)
                unit(g, 1)
            attend(KV_HEADS - 1, 0)

            def ffn_norm_stats(*tiles):
                layernorm_stats(4 * PAIRS + tiles[0], len(tiles), lambda j: xacc[:, tiles[j], :])

            def ffn_norm_apply(*tiles):
                if tiles[0] >= UTILES:
                    dve.wait_ge(tr_filled, TR_STAGE1 + tiles[-1] - UTILES + 1)
                layernorm_apply(4 * PAIRS + tiles[0], len(tiles), lambda j: xacc[:, tiles[j], :],
                                lambda j: ffn_norm[:, tiles[j] % UTILES, :])

            def ffn_gates(t):
                inner = FFN_MG[t][:, :].rearrange("p (i n) -> p i n", i=UTILES)

                def grid(a, axis):
                    return a.unsqueeze(axis).broadcast_to([P, UTILES, EXPERTS, EXPERTS])

                logits, centred, chosen, rank = (a[:, :, :] for a in (logit, g_exp, g_sel, g_rank))
                above, equal = cmp_gt[:, :, :, :], cmp_eq[:, :, :, :]
                dve.wait_ge(f_mg, UTILES * (t + 1))
                dve.tensor_copy(logits, inner[:, :, ER:ER + EXPERTS]).then_inc(f_logit, 1)
                dve.wait_ge(f_logit, t + 1)
                dve.tensor_reduce(g_max[:, :], logits, AX.X, ALU.max).then_inc(f_max, 1)
                tt(equal, grid(logits, 2), grid(logits, 3), ALU.is_equal).then_inc(f_cmp, 1)
                dve.wait_ge(f_max, t + 1)
                tt(centred, logits, g_max[:, :].unsqueeze(2).broadcast_to([P, UTILES, EXPERTS]),
                   ALU.subtract).then_inc(f_centred, 1)
                tt(above, grid(logits, 2), grid(logits, 3), ALU.is_gt)
                dve.wait_ge(f_cmp, 3 * t + 1)
                tt(equal, equal, con[:, C_TRIL:C_END].rearrange("p (e f) -> p e f", e=EXPERTS).unsqueeze(1)
                   .broadcast_to([P, UTILES, EXPERTS, EXPERTS]), ALU.mult).then_inc(f_cmp, 1)
                dve.wait_ge(f_cmp, 3 * t + 2)
                tt(above, above, equal, ALU.add).then_inc(f_cmp, 1)
                dve.wait_ge(f_cmp, 3 * t + 3)
                dve.tensor_reduce(rank, above, AX.X, ALU.add).then_inc(f_rank, 1)
                dve.wait_ge(f_exp, t + 1)
                dve.wait_ge(f_rank, t + 1)
                dve.scalar_tensor_tensor(out=chosen, in0=rank, scalar=1.5, in1=centred,
                                         op0=ALU.is_lt, op1=ALU.mult).then_inc(f_chosen, 1)
                dve.wait_ge(f_chosen, t + 1)
                if t:
                    dve.wait_ge(f_gT, t)
                tt(gated.rearrange("p i (e r) -> p i e r", e=EXPERTS),
                   inner[:, :, 0:ER].rearrange("p i (e r) -> p i e r", e=EXPERTS),
                   chosen.unsqueeze(3).broadcast_to([P, UTILES, EXPERTS, RANK]), ALU.mult).then_inc(f_gated, 1)
                dve.tensor_reduce(g_sum[:, :], chosen, AX.X, ALU.add).then_inc(f_sum, 1)
                dve.wait_ge(f_sum, t + 1)
                dve.reciprocal(g_inv[:, :], g_sum[:, :]).then_inc(f_inv, 1)
                dve.wait_ge(f_inv, t + 1)
                dve.tensor_scalar(g_scale[:, t * UTILES:(t + 1) * UTILES], g_inv[:, :], LORA_SCALE, None, ALU.mult).then_inc(f_scale, 1)

            def ffn_gT_lo(t):
                dve.wait_ge(f_gT_hi, t + 1)
                for i in range(2):
                    cols = slice(i * 2 * P, (i + 1) * 2 * P)
                    lo_part(gm_split[ER:P, cols], FFN_GT[t][0:ER, cols], gm_split[0:ER, cols]).then_inc(f_gT_lo, 1)

            def ffn_result(n):
                dve.wait_ge(f_y, n + 1)
                dve.wait_ge(f_scale, n // UTILES + 1)
                dve.scalar_tensor_tensor(out=xacc[:, n, :], in0=FFN_Y[n][:, :], scalar=g_scale[:, n:n + 1],
                                         in1=xacc[:, n, :], op0=ALU.mult, op1=ALU.add).then_inc(f_out, 1)

            def add_last(i):
                add_output(LAST, 1, i, LAST_OUT[i])

            cap_scores(LAST, 1, 0)
            find_max(LAST, 0)
            add_output(LAST - 1, 0, 0, RING[0])
            add_output(LAST - 1, 0, 1, RING[1])
            cap_scores(LAST, 1, 1)
            shift(LAST, 0)
            find_max(LAST, 1)
            shift(LAST, 1)
            normalise(LAST, 0)
            normalise(LAST, 1)
            probs_lo(LAST, 0)
            probs_lo(LAST, 1)
            dve.wait_ge(x_added, ADDED_1 + UTILES * (LAST - 1) + 2)
            ffn_norm_stats(0, 1)
            ffn_norm_apply(0, 1)
            output_lo(LAST, 0)
            output_lo(LAST, 1)
            add_output(LAST - 1, 0, 2, RING[2])
            add_output(LAST - 1, 0, 3, RING[3])
            dve.wait_ge(x_added, ADDED_1 + UTILES * LAST)
            ffn_norm_stats(2, 3)
            ffn_norm_apply(2, 3)
            add_last(0)
            add_last(1)
            dve.wait_ge(x_added, ADDED_1 + UTILES * LAST + 2)
            ffn_norm_stats(4, 5)
            ffn_norm_apply(4, 5)
            add_last(2)
            dve.wait_ge(x_added, ADDED_1 + UTILES * LAST + 3)
            ffn_norm_stats(6)
            ffn_norm_apply(6)
            add_last(3)
            dve.wait_ge(x_added, ADDED_1 + UTILES * LAST + 4)
            ffn_norm_stats(7)
            ffn_norm_apply(7)
            ffn_gates(0)
            ffn_gT_lo(0)
            ffn_gates(1)
            ffn_result(0)
            ffn_gT_lo(1)
            for n in range(1, TILES):
                ffn_result(n)

        @block.gpsimd
        def _(pool):
            def lo_part(dst_lo, value, hi):
                return pool.tensor_tensor(dst_lo, value, hi.bitcast(F32), ALU.subtract)

            def inverse_std_tiles(n, m):
                for j in range(m):
                    pool.wait_ge(ln_var, n + j + 1)
                    pool.tensor_tensor(rstd[:, j, :], var_eps[:, j, :], minus_half[:, :], ALU.pow).then_inc(ln_rstd, 1)

            def inverse_std(pair):
                inverse_std_tiles(2 * pair, 2)

            def split_wk(p):
                pool.wait_ge(wk_hi_done, p + 1)
                lo_part(wk_lo, wk_raw, wk_hi).then_inc(wk_split, 1)

            def add_bias(p):
                for j in range(2):
                    pool.wait_ge(ln_out, 2 * norm1_index(p) + j + 1)
                    rows = xacc[:, bass.ds(2 * p + j, 1), :].rearrange("p o e -> p (o e)")
                    pool.tensor_tensor(rows, rows, bias_bc, ALU.add).then_inc(biased, 1)

            def split_wv(p):
                pool.wait_ge(wv_hi_done, p)
                lo_part(wv_lo, wv_raw, wv_hi).then_inc(wv_split, 1)

            split_wk(0)
            pool.wait_ge(const_set, 1)
            pool.wait_ge(d_w, 16)
            pool.wait_ge(blocks_flagged, 1)
            w_blocks = w_rows.rearrange("p c (b k) -> p (c b) k", k=SPARSE_BLOCK)
            pool.tensor_tensor(w_blocks, w_blocks, block_sum[:, :, :].rearrange("p c b -> p (c b)").unsqueeze(2)
                               .broadcast_to([P, CH * (E // SPARSE_BLOCK), SPARSE_BLOCK]), ALU.mult).then_inc(w_masked, 1)
            inverse_std(norm1_index(0))
            split_wv(1)
            pool.wait_ge(d_bias, 16)
            add_bias(0)
            inverse_std(norm1_index(1))
            add_bias(1)
            inverse_std(norm2_index(0))
            with pool.Fori(1, PAIRS - 1) as p:
                inverse_std(norm1_index(p + 1))
                split_wk(p)
                add_bias(p + 1)
                inverse_std(norm2_index(p))
                split_wv(p + 1)
            split_wk(PAIRS - 1)

            def split_wq(g):
                for c in range(CH):
                    pool.wait_ge(wq_hi_done, CH * g + c + 1)
                    lo_part(wq_lo[:, c, :], wq_raw[:, c, :], wq_hi[:, c, :]).then_inc(wq_split, 1)

            def split_wo(g):
                for h in range(GROUP):
                    pool.wait_ge(wo_hi_done, GROUP * g + h + 1)
                    lo_part(wo_lo[:, h, :], wo_raw[:, h, :], wo_hi[:, h, :]).then_inc(wo_split, 1)

            split_wq(0)
            inverse_std(norm2_index(PAIRS - 1))
            with pool.Fori(0, KV_HEADS - 1) as g:
                split_wo(g)
                split_wq(g + 1)
            split_wo(KV_HEADS - 1)
            pool.wait_ge(b_hi_done, 1)
            lo_part(b_low, bT[:, :], b_twice[0:ER, :]).then_inc(b_split, 1)
            for first, count in ((0, 2), (2, 2), (4, 2), (6, 1), (7, 1)):
                inverse_std_tiles(4 * PAIRS + first, count)

INPUTS = ["x", "ctx_4096", "pos_BxS2", "mask_BxSxS2_ik0", "L0_attn_mask", "L0_attn_weight", "L0_attn_bias",
          "L0_xattn_Wq", "L0_xattn_Wk", "L0_xattn_Wv", "L0_xattn_Wo", "L0_ffn_A", "L0_ffn_B", "L0_ffn_Wr"]


def kernel(**inputs):
    import concourse.bacc as bacc
    from concourse.bass_utils import run_bass_kernel_spmd

    nc = bacc.Bacc("TRN2", target_bir_lowering=False, num_devices=1)
    arrays, args = {}, []
    for name in INPUTS:
        a = np.ascontiguousarray(inputs[name])
        arrays[f"in_{name}"] = a
        args.append(nc.dram_tensor(f"in_{name}", a.shape, mybir.dt.from_np(a.dtype), kind="ExternalInput").ap())
    arrays["in_constants"] = shape_constants()
    args.append(nc.dram_tensor("in_constants", (P, C_ALL), F32, kind="ExternalInput").ap())
    out = nc.dram_tensor("out_y", tuple(inputs["x"].shape), F32, kind="ExternalOutput").ap()
    decoder_layer(nc, *args, out)
    result = run_bass_kernel_spmd(nc, [arrays], core_ids=[0])
    return result.results[0]["out_y"]
```
